# Optimizing a Trainium2 kernel written in Bass

```python
import numpy as np
import jax
import jax.numpy as jnp

def _softmax(x, axis=-1):
    return jax.nn.softmax(x, axis=axis)

def _gelu(x):
    return jax.nn.gelu(x, approximate=True)

def _silu(x):
    return jax.nn.silu(x)

def _sigmoid(x):
    return jax.nn.sigmoid(x)

def _layernorm(x, axis=-1, eps=1e-05):
    m = jnp.mean(x, axis=axis, keepdims=True)
    v = jnp.var(x, axis=axis, keepdims=True)
    return (x - m) / jnp.sqrt(v + eps)

def _scatter_add(tgt, idx, src, axis=0):
    return tgt.at[idx].add(src)

def _segment_sum(src, seg, n):
    return jax.ops.segment_sum(src, seg, n)
kernel_name = 'mk_gnn_resnorm_d4_gnn_r64_be6ec7'

def setup_inputs(seed: int=0):
    np.random.seed(seed)
    _w = jnp.asarray

    def _rec_inputs():
        import jax
        import jax.numpy as jnp
        _gk = jax.random.key(seed)
        x = -0.000202 + 1 * jax.random.normal(jax.random.fold_in(_gk, 1), (50000, 128), jnp.float32)
        src = jax.random.randint(jax.random.fold_in(_gk, 2), (12500,), 0, 50000, jnp.int32)
        dst = jax.random.randint(jax.random.fold_in(_gk, 3), (12500,), 0, 50000, jnp.int32)
        _o = jnp.argsort(dst, stable=True)
        src = src[_o]
        dst = dst[_o]
        edge_attr_128 = 5.93493e-05 + 1.00006 * jax.random.normal(jax.random.fold_in(_gk, 12), (12500, 128), jnp.float32)
        edge_type_8 = jax.random.randint(jax.random.fold_in(_gk, 14), (12500,), 0, 8, jnp.int32)
        return (x, src, dst, edge_attr_128, edge_type_8)
    x, src, dst, edge_attr_128, edge_type_8 = _rec_inputs()

    def _L0_gnn_setup():
        import jax, jax.numpy as jnp
        import numpy as np
        N, E = (50000, 9375)
        ND, ED, HD = (128, 128, 128)
        EPS = 1e-05
        key = jax.random.key(seed)
        ks = jax.random.split(key, 8)
        w = lambda k, shape: jax.random.normal(k, shape, jnp.float32) * 0.05
        return {'node_features': jax.random.normal(ks[0], (N, ND), jnp.float32), 'edge_index': jax.random.randint(ks[1], (2, E), 0, N, jnp.int32), 'edge_attr': jax.random.normal(ks[2], (E, ED), jnp.float32), 'W1': w(ks[3], (2 * ND + ED, HD)), 'b1': jnp.zeros((HD,), jnp.float32), 'W2': w(ks[4], (HD, HD)), 'b2': jnp.zeros((HD,), jnp.float32), 'U1': w(ks[5], (ND + HD, HD)), 'ub1': jnp.zeros((HD,), jnp.float32), 'U2': w(ks[6], (HD, HD)), 'ub2': jnp.zeros((HD,), jnp.float32), 'gamma': jnp.ones((HD,), jnp.float32), 'beta': jnp.zeros((HD,), jnp.float32)}
    _L0_gnn_all = _L0_gnn_setup()
    _L0_gnn_in = {k: v for k, v in _L0_gnn_all.items() if k in ('W1', 'b1', 'W2', 'b2', 'U1', 'ub1', 'U2', 'ub2', 'gamma', 'beta')}
    del _L0_gnn_all

    def _L1_gnn_setup():
        import jax, jax.numpy as jnp
        import numpy as np
        N_NODES = 10000
        N_EDGES = 10000
        IN_FEATS = 128
        OUT_FEATS = 128
        key = jax.random.key(seed)
        k_x, k_w, k_b, k_row, k_col = jax.random.split(key, 5)
        x = jax.random.normal(k_x, (N_NODES, IN_FEATS), dtype=jnp.float32)
        W = jax.random.normal(k_w, (OUT_FEATS, 2 * IN_FEATS), dtype=jnp.float32) * 0.05
        b = jax.random.normal(k_b, (OUT_FEATS,), dtype=jnp.float32) * 0.05
        row = jax.random.randint(k_row, (N_EDGES,), 0, N_NODES)
        col = jax.random.randint(k_col, (N_EDGES,), 0, N_NODES)
        return {'x': x, 'W': W, 'b': b, 'row': row, 'col': col}
    _L1_gnn_all = _L1_gnn_setup()
    _L1_gnn_in = {k: v for k, v in _L1_gnn_all.items() if k in ('W', 'b')}
    del _L1_gnn_all

    def _L2_gnn_setup():
        import jax, jax.numpy as jnp
        import numpy as np
        N, E, D_IN, D_OUT, R = (50000, 12500, 128, 128, 8)
        key = jax.random.key(seed)
        ks = jax.random.split(key, 6)
        x = jax.random.normal(ks[0], (N, D_IN), dtype=jnp.float32)
        W_rel = jax.random.normal(ks[1], (R, D_IN, D_OUT), dtype=jnp.float32) * (1.0 / np.sqrt(D_IN))
        W_self_w = jax.random.normal(ks[2], (D_OUT, D_IN), dtype=jnp.float32) * (1.0 / np.sqrt(D_IN))
        W_self_b = jax.random.normal(ks[3], (D_OUT,), dtype=jnp.float32) * 0.01
        edge_index = jax.random.randint(ks[4], (2, E), 0, N, dtype=jnp.int32)
        edge_type = jax.random.randint(ks[5], (E,), 0, R, dtype=jnp.int32)
        return {'x': x, 'W_rel': W_rel, 'W_self_w': W_self_w, 'W_self_b': W_self_b, 'edge_index': edge_index, 'edge_type': edge_type}
    _L2_gnn_all = _L2_gnn_setup()
    _L2_gnn_in = {k: v for k, v in _L2_gnn_all.items() if k in ('W_rel', 'W_self_w', 'W_self_b')}
    del _L2_gnn_all

    def _L3_gnn_setup():
        import jax, jax.numpy as jnp
        import numpy as np
        N_NODES = 50000
        N_EDGES = 12500
        D_IN = 128
        D_OUT = 128
        key = jax.random.key(seed)
        ks = jax.random.split(key, 6)
        x = jax.random.normal(ks[0], (N_NODES, D_IN), dtype=jnp.float32)
        edge_index = jax.random.randint(ks[1], (2, N_EDGES), 0, N_NODES, dtype=jnp.int32)
        s1 = 1.0 / np.sqrt(2 * D_IN)
        s2 = 1.0 / np.sqrt(D_IN)
        W1 = jax.random.normal(ks[2], (2 * D_IN, D_IN), dtype=jnp.float32) * s1
        b1 = jnp.zeros((D_IN,), dtype=jnp.float32)
        W2 = jax.random.normal(ks[3], (D_IN, 1), dtype=jnp.float32) * s2
        b2 = jnp.zeros((1,), dtype=jnp.float32)
        Wl = jax.random.normal(ks[4], (D_IN, D_OUT), dtype=jnp.float32) * s2
        bl = jnp.zeros((D_OUT,), dtype=jnp.float32)
        return {'x': x, 'edge_index': edge_index, 'W1': W1, 'b1': b1, 'W2': W2, 'b2': b2, 'Wl': Wl, 'bl': bl}
    _L3_gnn_all = _L3_gnn_setup()
    _L3_gnn_in = {k: v for k, v in _L3_gnn_all.items() if k in ('W1', 'b1', 'W2', 'b2', 'Wl', 'bl')}
    del _L3_gnn_all
    return {'x': x, 'src': src, 'dst': dst, 'edge_attr_128': edge_attr_128, 'edge_type_8': edge_type_8, 'L0_gnn_W1': _L0_gnn_in['W1'], 'L0_gnn_b1': _L0_gnn_in['b1'], 'L0_gnn_W2': _L0_gnn_in['W2'], 'L0_gnn_b2': _L0_gnn_in['b2'], 'L0_gnn_U1': _L0_gnn_in['U1'], 'L0_gnn_ub1': _L0_gnn_in['ub1'], 'L0_gnn_U2': _L0_gnn_in['U2'], 'L0_gnn_ub2': _L0_gnn_in['ub2'], 'L0_gnn_gamma': _L0_gnn_in['gamma'], 'L0_gnn_beta': _L0_gnn_in['beta'], 'L1_gnn_W': _L1_gnn_in['W'], 'L1_gnn_b': _L1_gnn_in['b'], 'L2_gnn_W_rel': _L2_gnn_in['W_rel'], 'L2_gnn_W_self_w': _L2_gnn_in['W_self_w'], 'L2_gnn_W_self_b': _L2_gnn_in['W_self_b'], 'L3_gnn_W1': _L3_gnn_in['W1'], 'L3_gnn_b1': _L3_gnn_in['b1'], 'L3_gnn_W2': _L3_gnn_in['W2'], 'L3_gnn_b2': _L3_gnn_in['b2'], 'L3_gnn_Wl': _L3_gnn_in['Wl'], 'L3_gnn_bl': _L3_gnn_in['bl']}

def reference(x, src, dst, edge_attr_128, edge_type_8, L0_gnn_W1, L0_gnn_b1, L0_gnn_W2, L0_gnn_b2, L0_gnn_U1, L0_gnn_ub1, L0_gnn_U2, L0_gnn_ub2, L0_gnn_gamma, L0_gnn_beta, L1_gnn_W, L1_gnn_b, L2_gnn_W_rel, L2_gnn_W_self_w, L2_gnn_W_self_b, L3_gnn_W1, L3_gnn_b1, L3_gnn_W2, L3_gnn_b2, L3_gnn_Wl, L3_gnn_bl):
    import jax
    import jax.numpy as jnp

    def _L0_gnn_ref(node_features, edge_index, edge_attr, W1, b1, W2, b2, U1, ub1, U2, ub2, gamma, beta):
        import jax, jax.numpy as jnp
        import numpy as np
        N, E = (50000, 9375)
        ND, ED, HD = (128, 128, 128)
        EPS = 1e-05
        row, col = (edge_index[0], edge_index[1])
        edge_features = jnp.concatenate([node_features[row], node_features[col], edge_attr], axis=-1)
        messages = jax.nn.softplus(edge_features @ W1 + b1) @ W2 + b2
        aggregated = jax.ops.segment_sum(messages, row, num_segments=node_features.shape[0])
        combined = jnp.concatenate([node_features, aggregated], axis=-1)
        updated = jax.nn.softplus(combined @ U1 + ub1) @ U2 + ub2
        mu = jnp.mean(updated, axis=0)
        var = jnp.var(updated, axis=0)
        return (updated - mu) * jax.lax.rsqrt(var + EPS) * gamma + beta

    def _L1_gnn_ref(x, W, b, row, col):
        import jax, jax.numpy as jnp
        import numpy as np
        N_NODES = 10000
        N_EDGES = 10000
        IN_FEATS = 128
        OUT_FEATS = 128
        n = x.shape[0]
        deg = jax.ops.segment_sum(jnp.ones((row.shape[0],), dtype=x.dtype), row, num_segments=n)
        agg = jax.ops.segment_sum(x[col], row, num_segments=n)
        mean = agg / jnp.maximum(deg, 1.0)[:, None]
        h = jnp.concatenate([x, mean], axis=-1)
        out = h @ W.T + b
        return out

    def _L2_gnn_ref(x, W_rel, W_self_w, W_self_b, edge_index, edge_type):
        import jax, jax.numpy as jnp
        import numpy as np
        N, E, D_IN, D_OUT, R = (50000, 12500, 128, 128, 8)
        n = x.shape[0]
        out = x @ W_self_w.T + W_self_b
        src = edge_index[0]
        dst = edge_index[1]
        h = jnp.einsum('nd,rdo->rno', x, W_rel)
        msg = h[edge_type, src]
        agg = jax.ops.segment_sum(msg, dst, num_segments=n)
        deg = jax.ops.segment_sum(jnp.ones_like(dst, dtype=x.dtype), dst, num_segments=n)
        deg = jnp.maximum(deg, 1.0)[:, None]
        out = jax.nn.relu(out + agg / deg)
        return out

    def _L3_gnn_ref(x, edge_index, W1, b1, W2, b2, Wl, bl):
        import jax, jax.numpy as jnp
        import numpy as np
        N_NODES = 50000
        N_EDGES = 12500
        D_IN = 128
        D_OUT = 128
        row, col = (edge_index[0], edge_index[1])
        n, d = x.shape
        xc = x[row]
        xn = x[col]
        h = jax.nn.relu(xc @ W1[:d] + xn @ W1[d:] + b1)
        mask = jax.nn.sigmoid(h @ W2 + b2)[:, 0]
        seg_sum = jax.ops.segment_sum(mask, row, num_segments=n)
        w = mask / (seg_sum[row] + 1e-09)
        agg = jax.ops.segment_sum(w[:, None] * xn, row, num_segments=n)
        deg = jax.ops.segment_sum(jnp.ones_like(mask), row, num_segments=n)
        out_emb = jnp.where((deg > 0)[:, None], 0.5 * x + 0.5 * agg, x)
        return jax.nn.relu(out_emb @ Wl + bl)
    edge_index = jnp.stack([src, dst])
    x = _layernorm(x + _L0_gnn_ref(x, edge_index, edge_attr_128, L0_gnn_W1, L0_gnn_b1, L0_gnn_W2, L0_gnn_b2, L0_gnn_U1, L0_gnn_ub1, L0_gnn_U2, L0_gnn_ub2, L0_gnn_gamma, L0_gnn_beta), axis=-1)
    x = _layernorm(x + _L1_gnn_ref(x, L1_gnn_W, L1_gnn_b, src, dst), axis=-1)
    x = _layernorm(x + _L2_gnn_ref(x, L2_gnn_W_rel, L2_gnn_W_self_w, L2_gnn_W_self_b, edge_index, edge_type_8), axis=-1)
    x = _layernorm(x + _L3_gnn_ref(x, edge_index, L3_gnn_W1, L3_gnn_b1, L3_gnn_W2, L3_gnn_b2, L3_gnn_Wl, L3_gnn_bl), axis=-1)
    return x

_drawn_inputs = setup_inputs


def setup_inputs(seed=0):
    import zlib

    import numpy as np

    out = dict(_drawn_inputs(seed))
    spreads = {'L0_gnn_b1': (0.0, 0.658),
     'L0_gnn_b2': (0.0, 0.3),
     'L0_gnn_ub1': (0.0, 0.1),
     'L0_gnn_ub2': (0.0, 2.0),
     'L0_gnn_gamma': (1.0, 0.2),
     'L0_gnn_beta': (0.0, 0.1),
     'L3_gnn_b1': (0.0, 2.0),
     'L3_gnn_bl': (0.0, 0.1)}
    factors = {'L2_gnn_W_self_b': 8.0, 'L3_gnn_W1': 8.0, 'L3_gnn_W2': 8.0}
    for name, (base, spread) in spreads.items():
        noise = np.random.default_rng([zlib.crc32(name.encode()), seed]).standard_normal(out[name].shape)
        drawn = base * np.exp(spread * noise) if base else spread * noise
        out[name] = jnp.asarray(drawn.astype(out[name].dtype))
    for name, factor in factors.items():
        out[name] = (out[name] * factor).astype(out[name].dtype)
    return out
```

```python
import concourse.bass as bass
from concourse import mybir
from contextlib import ExitStack

F32, BF16, I32, U32 = mybir.dt.float32, mybir.dt.bfloat16, mybir.dt.int32, mybir.dt.uint32
ALU = mybir.AluOpType
ACT = mybir.ActivationFunctionType

N, E, D, R = 50000, 12500, 128, 8
P, T = 125, 4
B = P * T
G = E // B
AW = 132
SINK = B
EPS = 1e-5
TABLES = "natural_log_exp_and_others"
Q = N // G // B


def nth(amount, g, par):
    return (g - par) * (amount // 2) + amount


def each_step(eng, step, n=G):
    step(0, 0)
    step(1, 1)
    with eng.Fori(2, n - 1, 2) as g:
        step(g, 0)
        step(g + 1, 1)
    step(n - 1, 0)


def index(ap):
    return bass.IndirectOffsetOnAxis(ap=ap, axis=0)


def settled(eng, began):
    eng.sem_inc(began, 1)


class Store:
    pass


def allocate(nc, m, ctx, prefix):
    m.spent, m.fresh = m.spent + m.fresh, []

    def sb(name, shape, dt=F32):
        return ctx.enter_context(nc.sbuf_tensor(f"{prefix}_{name}", shape, dt))

    def sem(name):
        m.fresh.append(ctx.enter_context(nc.semaphore(f"{prefix}_{name}")))
        return m.fresh[-1]

    def pool_sem(name):
        return m.ctx.enter_context(nc.semaphore(f"{prefix}_{name}"))
    return sb, sem, pool_sem


def clear_spent(pool, m):
    for signal in m.spent:
        pool.sem_clear(signal)
    m.spent = []


def split_row(nc, dve, link, m, row, dst, tmp_b, tmp_f):
    link(nc.vector.tensor_copy(tmp_b[:, 0:D], row))
    link(nc.vector.tensor_tensor(tmp_f[:, 0:D], row, tmp_b[:, 0:D], ALU.subtract))
    link(nc.vector.tensor_copy(tmp_b[:, D:2 * D], tmp_f[:, 0:D]))
    link(nc.vector.tensor_tensor(tmp_f[:, D:2 * D], tmp_f[:, 0:D], tmp_b[:, D:2 * D], ALU.subtract))
    link(nc.vector.tensor_scalar(tmp_f[:, 0:D], tmp_b[:, 0:D], m.ident[:, 0:1], None, ALU.mult))
    link(nc.vector.scalar_tensor_tensor(tmp_f[:, 0:D], tmp_b[:, D:2 * D], m.ident[:, 1:2], tmp_f[:, 0:D],
                                        ALU.mult, ALU.add))
    link(nc.vector.scalar_tensor_tensor(tmp_f[:, 0:D], tmp_f[:, D:2 * D], m.ident[:, 2:3], tmp_f[:, 0:D],
                                        ALU.mult, ALU.add))
    for c in range(T):
        link(nc.vector.tensor_copy(dst[:, c * D:(c + 1) * D], tmp_f[:, 0:D]))


def setup(nc, m, a):
    with ExitStack() as ctx:
        sb, sem, pool_sem = allocate(nc, m, ctx, "setup")
        raw = sb("raw", [128, 3, D])
        tmp_b = sb("tmp_b", [128, 2 * D], BF16)
        tmp_f = sb("tmp_f", [128, 2 * D])
        rows = sb("rows", [128, 4, D])
        pat = sb("pat", [P, T], I32)
        pat8 = sb("pat8", [P, R], I32)
        loaded, raw_in, rows_in = sem("loaded"), sem("raw_in"), sem("rows_in")
        made, turned, chain = sem("made"), sem("turned"), sem("chain")
        n_loads = 0
        block = ctx.enter_context(nc.Block())

        @block.sync
        def _(sp):
            nonlocal n_loads
            sp.dma_start(raw[:, 0, :], a["L1_gnn_W"][:, 0:D]).then_inc(raw_in, 16)
            sp.dma_start(raw[:, 1, :], a["L1_gnn_W"][:, D:2 * D]).then_inc(raw_in, 16)
            sp.dma_start(raw[:, 2, :], a["L2_gnn_W_self_w"][:, :]).then_inc(raw_in, 16)
            for i, b in enumerate(("L0_gnn_b2", "L1_gnn_b", "L2_gnn_W_self_b", "L3_gnn_bl")):
                sp.dma_start(rows[:, i, :], a[b].partition_broadcast(128)).then_inc(rows_in, 16)
            for dst, src in (
                    (m.w1[:, :, :], a["L0_gnn_W1"].rearrange("(c p) n -> p c n", p=D)),
                    (m.w2[:, :], a["L0_gnn_W2"][:, :]),
                    (m.u1[:, :, :], a["L0_gnn_U1"].rearrange("(c p) n -> p c n", p=D)),
                    (m.u2[:, :], a["L0_gnn_U2"][:, :]),
                    (m.wrel[:, :, :], a["L2_gnn_W_rel"].rearrange("r p n -> p r n")),
                    (m.v1[:, :, :], a["L3_gnn_W1"].rearrange("(c p) n -> p c n", p=D)),
                    (m.v2[:, :], a["L3_gnn_W2"][:, :]),
                    (m.wl[:, :], a["L3_gnn_Wl"][:, :]),
                    (m.nb2[:, :], a["L3_gnn_b2"].partition_broadcast(128))):
                sp.dma_start(dst, src).then_inc(loaded, 16)
                n_loads += 1
            for i, b in enumerate(m.columns):
                sp.dma_start(m.col[:, i:i + 1], a[b].rearrange("(p n) -> p n", n=1)).then_inc(loaded, 16)
                n_loads += 1
            sp.wait_ge(loaded, 16 * n_loads)

        @block.gpsimd
        def _(pool):
            clear_spent(pool, m)

            nc.gpsimd.memset(m.ident[:, :], 0.0).then_inc(made, 1)
            nc.gpsimd.memset(m.before[:, :], 1.0).then_inc(made, 1)
            nc.gpsimd.memset(m.ones3[:, :], 0.0).then_inc(made, 1)
            nc.gpsimd.memset(m.ones[:, :], 1.0).then_inc(made, 1)
            nc.gpsimd.iota(pat[:, :], pattern=[[P, T]], base=N, channel_multiplier=1).then_inc(made, 1)
            nc.gpsimd.iota(pat8[:, :], pattern=[[1, R]], base=0, channel_multiplier=0).then_inc(made, 1)
            pool.wait_ge(made, 6)
            nc.gpsimd.affine_select(out=m.ident[:, :], in_=m.ident[:, :], compare_op=ALU.not_equal, fill=1.0,
                                    base=0, pattern=[[-1, D]], channel_multiplier=1).then_inc(made, 1)
            nc.gpsimd.affine_select(out=m.before[:, :], in_=m.before[:, :], compare_op=ALU.is_gt, fill=0.0,
                                    base=0, pattern=[[1, P]], channel_multiplier=-1).then_inc(made, 1)
            nc.gpsimd.memset(m.ones3[0:3, :], 1.0).then_inc(made, 1)

        @block.vector
        def _(dve):
            n = 0

            def link(ins):
                nonlocal n
                n += 1
                ins.then_inc(chain, 1)
                dve.wait_ge(chain, n)
            link(nc.vector.memset(m.zero[:, :], 0.0))
            link(nc.vector.memset(m.eps[:, :], EPS))
            dve.wait_ge(made, 9)
            link(nc.vector.tensor_copy(m.sink[:, :], pat[:, :]))
            link(nc.vector.tensor_copy(m.relation[:, :], pat8[:, :]))
            link(nc.vector.memset(m.corr[:, :], 0.0))
            for l in range(1, 4):
                link(nc.vector.memset(m.xb[l][0][:, :, :], 0.0))
            dve.wait_ge(rows_in, 64)
            for i, dst in enumerate((m.b2row, m.l1row, m.l2row, m.l3row)):
                split_row(nc, dve, link, m, rows[:, i, :], dst, tmp_b, tmp_f)
            dve.wait_ge(loaded, 16 * 20 - 16 * (20 - n_loads))
            link(nc.vector.tensor_scalar(m.nb2[:, :], m.nb2[:, :], -1.0, None, ALU.mult))
            dve.wait_ge(turned, 3)
            link(nc.vector.tensor_copy(m.l1w[:, :, :], m.pm[0][:, 0:2 * D].rearrange("p (c n) -> p c n", c=2)))
            link(nc.vector.tensor_copy(m.l2w[:, :], m.pm[0][:, 2 * D:3 * D]))

        @block.tensor
        def _(pe):
            pe.wait_ge(raw_in, 48)
            pe.wait_ge(made, 9)
            for i in range(3):
                nc.tensor.transpose(m.pm[0][:, i * D:(i + 1) * D], raw[:, i, :], m.ident[:, :]).then_inc(turned, 1)


class Dedupe:

    def __init__(self, nc, m, sb, sem, lead):
        self.nc, self.m, self.lead = nc, m, lead
        self.key = sb("key", [P, T])
        self.diag = sb("diag", [P, T, P])
        self.krow = sb("krow", [P, B])
        self.same = sb("same", [P, T, B])
        self.key_done, self.diag_done = sem("key_done"), sem("diag_done")
        self.krow_mm, self.krow_copied = sem("krow_mm"), sem("krow_copied")
        self.same_done, self.sum_mm, self.sum_copied = sem("same_done"), sem("sum_mm"), sem("sum_copied")
        if lead:
            self.early = sb("early", [P, T, P])
            self.off = sb("off", [P, T])
            self.lidx = [sb(f"lidx{i}", [P, T], U32) for i in range(2)]
            self.early_done, self.cnt_mm = sem("early_done"), sem("cnt_mm")
            self.off_done, self.lidx_done = sem("off_done"), sem("lidx_done")

    def dve_diag(self, dve, g, ids):
        nc, m = self.nc, self.m
        if self.lead:
            dve.wait_ge(self.lidx_done, g)
        dve.wait_ge(self.same_done, g)
        nc.vector.tensor_copy(self.key[:, :], ids).then_inc(self.key_done, 1)
        dve.wait_ge(self.key_done, g + 1)
        dve.wait_ge(self.krow_mm, g)
        for j in range(T):
            last = nc.vector.tensor_scalar(self.diag[:, j, :], m.ident[0:P, 0:P], self.key[:, j:j + 1], None, ALU.mult)
        last.then_inc(self.diag_done, 1)

    def pe_krow(self, pe, g):
        nc, m = self.nc, self.m
        pe.wait_ge(self.diag_done, g + 1)
        pe.wait_ge(self.krow_copied, g)
        if self.lead:
            pe.wait_ge(self.lidx_done, g)
        nc.tensor.matmul(m.pk[0:P, 0:B], m.ones[0:P, 0:P], self.diag[:, :, :].rearrange("p a b -> p (a b)"),
                         start=True, stop=True).then_inc(self.krow_mm, 1)

    def act_krow(self, act, g):
        act.wait_ge(self.krow_mm, g + 1)
        act.wait_ge(self.same_done, g)
        self.nc.scalar.copy(self.krow[:, :], self.m.pk[0:P, 0:B]).then_inc(self.krow_copied, 1)

    def dve_same(self, dve, g):
        nc, m = self.nc, self.m
        dve.wait_ge(self.krow_copied, g + 1)
        dve.wait_ge(self.sum_mm, g)
        for j in range(T):
            last = nc.vector.tensor_scalar(self.same[:, j, :], self.krow[:, :], self.key[:, j:j + 1], None, ALU.is_equal)
        last.then_inc(self.same_done, 1)
        if self.lead:
            dve.wait_ge(self.same_done, g + 1)
            dve.wait_ge(self.cnt_mm, g)
            for j in range(T):
                last = nc.vector.tensor_tensor(self.early[:, j, :], self.same[:, j, j * P:(j + 1) * P],
                                               m.before[:, :], ALU.mult)
            last.then_inc(self.early_done, 1)

    def pe_count(self, pe, g):
        nc, m = self.nc, self.m
        pe.wait_ge(self.early_done, g + 1)
        pe.wait_ge(self.krow_copied, g + 1)
        for i in range(T):
            for j in range(i + 1):
                lhs = self.early[:, i, :] if i == j else self.same[:, j, i * P:(i + 1) * P]
                last = nc.tensor.matmul(m.pk[0:P, i:i + 1], lhs, m.ones[0:P, 0:1], start=(j == 0), stop=(j == i))
        last.then_inc(self.cnt_mm, 1)

    def dve_lead(self, dve, g, par, stored):
        nc, m = self.nc, self.m
        nc.vector.tensor_tensor(self.off[:, :], m.sink[:, :], self.key[:, :], ALU.subtract).then_inc(self.off_done, 1)
        dve.wait_ge(self.cnt_mm, g + 1)
        dve.wait_ge(self.off_done, 3 * g + 1)
        nc.vector.scalar_tensor_tensor(self.off[:, :], m.pk[0:P, 0:T], 0.5, self.off[:, :], ALU.is_gt,
                                       ALU.mult).then_inc(self.off_done, 1)
        dve.wait_ge(self.off_done, 3 * g + 2)
        nc.vector.tensor_tensor(self.off[:, :], self.off[:, :], self.key[:, :], ALU.add).then_inc(self.off_done, 1)
        dve.wait_ge(self.off_done, 3 * g + 3)
        dve.wait_ge(stored, nth(16, g, par) - 16)
        nc.vector.tensor_copy(self.lidx[par][:, :], self.off[:, :]).then_inc(self.lidx_done, 1)

    def pe_sum(self, pe, g, rhs, width):
        nc, m = self.nc, self.m
        pe.wait_ge(self.same_done, g + 1)
        pe.wait_ge(self.sum_copied, 2 * g)
        for i in range(T):
            for j in range(T):
                last = nc.tensor.matmul(m.pa[i // 2][0:P, (i % 2) * AW:(i % 2) * AW + width],
                                        self.same[:, j, i * P:(i + 1) * P], rhs(j), start=(j == 0), stop=(j == T - 1))
        last.then_inc(self.sum_mm, 1)

    def act_sum(self, act, g, dst, width):
        act.wait_ge(self.sum_mm, g + 1)
        for i in range(2):
            self.nc.scalar.copy(dst[:, 2 * i:2 * i + 2, 0:width],
                                self.m.pa[i][0:P, 0:2 * AW].rearrange("p (c n) -> p c n", c=2)[:, :, 0:width]
                                ).then_inc(self.sum_copied, 1)


def act_softplus(nc, act, exp_done, n, z, buf, bias):
    nc.scalar.activation(buf, z, ACT.Exp, bias=bias).then_inc(exp_done, 1)
    act.wait_ge(exp_done, n)
    return nc.scalar.activation(buf, buf, ACT.Ln, bias=1.0)


def dve_softplus(nc, dve, low_done, n, z, buf, bias):
    nc.vector.tensor_scalar(buf, buf, 40.0, None, ALU.min).then_inc(low_done, 1)
    dve.wait_ge(low_done, n)
    return nc.vector.scalar_tensor_tensor(buf, z, bias, buf, ALU.add, ALU.max)


def edges_mlp(nc, m, a):
    with ExitStack() as ctx:
        sb, sem, pool_sem = allocate(nc, m, ctx, "p0")
        ids = [sb(f"ids{i}", [P, 2 * T], I32) for i in range(2)]
        gx = [sb(f"gx{i}", [P, 2 * T, D]) for i in range(2)]
        ea = [sb(f"ea{i}", [P, T, D]) for i in range(2)]
        dx = [sb(f"dx{i}", [P, 4 * T, D]) for i in range(2)]
        xT = [sb(f"xT{i}", [128, B]) for i in range(7)]
        hid = sb("hid", [128, B])
        dhid = [[sb(f"dhid{i}{q}", [128, B]) for q in range(Q)] for i in range(2)]
        msg = sb("msg", [P, T, AW])
        out = [sb(f"out{i}", [P, T, AW]) for i in range(2)]
        ids_in = [sem(f"ids_in{i}") for i in range(2)]
        src_in = [pool_sem(f"src_in{i}") for i in range(2)]
        dst_in = [pool_sem(f"dst_in{i}") for i in range(2)]
        ea_in = [sem(f"ea_in{i}") for i in range(2)]
        dx_in = [sem(f"dx_in{i}") for i in range(2)]
        x_stored = [sem(f"x_stored{i}") for i in range(2)]
        h_stored = [sem(f"h_stored{i}") for i in range(2)]
        lead_stored = [sem(f"lead_stored{i}") for i in range(2)]
        cleared, cleared_next, summed = sem("cleared"), sem("cleared_next"), pool_sem("summed")
        t_done, t_copied = sem("t_done"), sem("t_copied")
        mm_done, mm_read = sem("mm_done"), sem("mm_read")
        exp_done, ln_done, low_done, prepared = sem("exp_done"), sem("ln_done"), sem("low_done"), sem("prepared")
        sp_began, pool_began = sem("sp_began"), sem("pool_began")
        dd = Dedupe(nc, m, sb, sem, lead=True)
        J, K = 7, 10
        HID = {0: 0, 1: 1, 2: 2, 3: 3, 5: 4}
        NODE = {1: 0, 2: 1, 3: 2, 5: 3}
        XB = (m.b_b1, m.b_ub1)
        src_v, dst_v = (a[k].rearrange("(p t) -> p t", p=P) for k in ("src", "dst"))
        ea_v = a["edge_attr_128"].rearrange("(p t) n -> p t n", p=P)
        x_v = a["x"].rearrange("(g p r) n -> g p (r n)", p=P, r=4 * T)
        zero_v = [t[0:N, :].rearrange("(g p r) n -> g p (r n)", p=P, r=16) for t in m.table]
        block = ctx.enter_context(nc.Block())

        @block.sync
        def _(sp):
            def until(signal, value):
                sp.wait_ge(signal, value)
                settled(sp, sp_began)

            def load(g, par):
                until(src_in[par], nth(64, g, par) - 64)
                until(dst_in[par], nth(64, g, par) - 64)
                if not (isinstance(g, int) and g < 2):
                    until(dd.key_done, g - 1)
                    until(t_done, J * (g - 1))
                sp.dma_start(ids[par][:, 0:T], src_v[:, bass.ds(T * g, T)]).then_inc(ids_in[par], 16)
                sp.dma_start(ids[par][:, T:2 * T], dst_v[:, bass.ds(T * g, T)]).then_inc(ids_in[par], 16)
                sp.dma_start(ea[par][:, :, :], ea_v[:, bass.ds(T * g, T), :]).then_inc(ea_in[par], 16)
                for lo, hi in ((0, 112), (112, P)):
                    sp.dma_start(dx[par][lo:hi, :, :].rearrange("p r n -> p (r n)"),
                                 x_v[bass.ds(g, 1), lo:hi, :].rearrange("g p n -> (g p) n")).then_inc(dx_in[par], 16)

            def store(g, par):
                until(src_in[par], nth(64, g, par))
                until(dst_in[par], nth(64, g, par))
                sp.dma_start(m.state[0][bass.ds(g, 1), :, :].rearrange("g p n -> (g p) n"),
                             gx[par][:, :, :].rearrange("p t n -> p (t n)")).then_inc(x_stored[par], 16)
                sp.dma_start(zero_v[1][bass.ds(g, 1), :, :].rearrange("g p n -> (g p) n"),
                             m.zero[0:P, :]).then_inc(cleared_next, 16)
                for k, q in NODE.items():
                    until(mm_read, K * g + k + 3)
                    sp.dma_start(m.hidden[bass.ds(Q * g + q, 1), :, :].rearrange("g p n -> (g p) n"),
                                 dhid[par][q][:, :]).then_inc(h_stored[par], 16)
                until(dd.lidx_done, g + 1)
                sp.dma_start(m.lead[0][bass.ds(g, 1), :, :].rearrange("g p n -> (g p) n"),
                             dd.lidx[par][:, :].bitcast(I32)).then_inc(lead_stored[par], 16)
            load(0, 0)
            load(1, 1)
            for g in range(G):
                sp.dma_start(zero_v[0][g], m.zero[0:P, :]).then_inc(cleared, 16)
            for t in m.table:
                sp.dma_start(t[N:N + SINK, :].rearrange("(p r) n -> p (r n)", p=P),
                             m.zero[0:P, 0:T * AW]).then_inc(cleared, 16)
            with sp.Fori(0, G - 3, 2) as g:
                store(g, 0)
                load(g + 2, 0)
                store(g + 1, 1)
                load(g + 3, 1)
            store(G - 3, 0)
            load(G - 1, 0)
            store(G - 2, 1)
            store(G - 1, 0)
            for par, n in ((0, (G + 1) // 2), (1, G // 2)):
                sp.wait_ge(x_stored[par], 16 * n)
                sp.wait_ge(h_stored[par], 64 * n)
                sp.wait_ge(lead_stored[par], 16 * n)
            sp.wait_ge(cleared_next, 16 * G)

        @block.gpsimd
        def _(pool):
            clear_spent(pool, m)

            def gather(g, par):
                pool.wait_ge(ids_in[par], nth(32, g, par))
                pool.wait_ge(x_stored[par], nth(16, g, par) - 16)
                if not (isinstance(g, int) and g < 2):
                    pool.wait_ge(t_done, J * (g - 1))
                settled(pool, pool_began)
                for s, got in ((0, src_in), (1, dst_in)):
                    for j in range(T):
                        k = T * s + j
                        pool.indirect_dma_start(out=gx[par][:, k, :], out_offset=None, in_=a["x"][:, :],
                                                in_offset=index(ids[par][:, k:k + 1].bitcast(U32))
                                                ).then_inc(got[par], 16)

            def scatter(g, par):
                pool.wait_ge(dd.lidx_done, g + 1)
                pool.wait_ge(dd.sum_copied, 2 * (g + 1))
                pool.wait_ge(summed, 64 * g)
                settled(pool, pool_began)
                for j in range(T):
                    pool.indirect_dma_start(out=m.table[0][:, :], out_offset=index(dd.lidx[par][:, j:j + 1]),
                                            in_=out[par][:, j, :], in_offset=None, compute_op=ALU.add
                                            ).then_inc(summed, 16)
            gather(0, 0)
            gather(1, 1)
            pool.wait_ge(cleared, 16 * (G + 4))
            scatter(0, 0)
            with pool.Fori(2, G - 1, 2) as g:
                gather(g, 0)
                scatter(g - 1, 1)
                gather(g + 1, 1)
                scatter(g, 0)
            gather(G - 1, 0)
            scatter(G - 2, 1)
            scatter(G - 1, 0)
            pool.wait_ge(summed, 64 * G)

        @block.tensor
        def _(pe):
            def turn(g, par, k, tiles):
                pe.wait_ge(t_copied, J * g + k + 1)
                bank = m.pt[(par * J + k) % 2]
                for j in range(T):
                    last = nc.tensor.transpose(bank[:, j * P:(j + 1) * P], tiles(j), m.ident[0:P, 0:P])
                last.then_inc(t_done, 1)

            def product(g, k):
                pe.wait_ge(mm_read, K * g + k + 1)
                return m.pm[k % 2]

            def node_hidden(g, k):
                q = NODE[k]
                pe.wait_ge(t_copied, J * g + 3 + q + 3)
                bank = product(g, k)
                nc.tensor.matmul(bank[:, 0:B], m.u1[:, 0, :], xT[3 + q][:, :], start=True, stop=True).then_inc(mm_done, 1)

            def step(g, par):
                pe.wait_ge(src_in[par], nth(64, g, par))
                turn(g, par, 0, lambda j: gx[par][:, j, :])
                pe.wait_ge(dst_in[par], nth(64, g, par))
                turn(g, par, 1, lambda j: gx[par][:, T + j, :])
                pe.wait_ge(ea_in[par], nth(16, g, par))
                turn(g, par, 2, lambda j: ea[par][:, j, :])
                pe.wait_ge(dx_in[par], nth(32, g, par))
                turn(g, par, 3, lambda j: dx[par][:, j, :])
                pe.wait_ge(t_copied, J * g + 2 + 3)
                bank = product(g, 0)
                for c in range(3):
                    last = nc.tensor.matmul(bank[:, 0:B], m.w1[:, c, :], xT[c][:, :], start=(c == 0), stop=(c == 2))
                last.then_inc(mm_done, 1)
                dd.pe_krow(pe, g)
                turn(g, par, 4, lambda j: dx[par][:, T + j, :])
                node_hidden(g, 1)
                turn(g, par, 5, lambda j: dx[par][:, 2 * T + j, :])
                node_hidden(g, 2)
                turn(g, par, 6, lambda j: dx[par][:, 3 * T + j, :])
                node_hidden(g, 3)
                pe.wait_ge(mm_read, K * g + 0 + 3)
                bank = product(g, 4)
                nc.tensor.matmul(bank[0:P, :], m.ones3[:, 0:P], m.b2row[:, :], start=True, stop=False)
                for j in range(T):
                    last = nc.tensor.matmul(bank[0:P, j * D:(j + 1) * D], hid[:, j * P:(j + 1) * P], m.w2[:, :],
                                            start=False, stop=(j == T - 1))
                last.then_inc(mm_done, 1)
                node_hidden(g, 5)
                dd.pe_count(pe, g)
                pe.wait_ge(mm_read, K * g + 4 + 3)
                dd.pe_sum(pe, g, lambda j: msg[:, j, :], AW)
                for k, q in NODE.items():
                    pe.wait_ge(mm_read, K * g + k + 3)
                    bank = product(g, 6 + q)
                    nc.tensor.matmul(bank[:, 0:B], m.u2[:, :], dhid[par][q][:, :], start=True,
                                     stop=True).then_inc(mm_done, 1)
            each_step(pe, step)

        @block.scalar
        def _(act):
            nc.scalar.preload_act_table_set(TABLES)
            act.sem_inc(t_copied, 2)

            def copy(g, par, k):
                act.wait_ge(t_done, J * g + k + 1)
                act.wait_ge(mm_done, K * g)
                nc.scalar.copy(xT[k][:, :], m.pt[(par * J + k) % 2][:, 0:B]).then_inc(t_copied, 1)

            def softplus(g, k, buf, bias):
                act.wait_ge(mm_done, K * g + k + 1)
                act_softplus(nc, act, exp_done, 5 * g + HID[k] + 1, m.pm[k % 2][:, 0:B], buf, bias
                             ).then_inc(ln_done, 1)

            def step(g, par):
                for k in range(4):
                    copy(g, par, k)
                softplus(g, 0, hid[:, :], m.b_b1)
                dd.act_krow(act, g)
                act.wait_ge(h_stored[par], nth(64, g, par) - 64)
                copy(g, par, 4)
                softplus(g, 1, dhid[par][0][:, :], m.b_ub1)
                copy(g, par, 5)
                softplus(g, 2, dhid[par][1][:, :], m.b_ub1)
                copy(g, par, 6)
                softplus(g, 3, dhid[par][2][:, :], m.b_ub1)
                softplus(g, 5, dhid[par][3][:, :], m.b_ub1)
                if not (isinstance(g, int) and g < 2):
                    act.wait_ge(summed, 64 * (g - 1))
                dd.act_sum(act, g, out[par], AW)
            each_step(act, step)

        @block.vector
        def _(dve):
            dve.sem_inc(mm_read, 2)
            nc.vector.memset(msg[:, :, D:AW], 0.0).then_inc(prepared, 1)
            dve.wait_ge(prepared, 1)
            nc.vector.memset(msg[:, :, D:D + 1], 1.0).then_inc(prepared, 1)

            def finish(g, k, buf, bias):
                dve.wait_ge(ln_done, 5 * g + HID[k] + 1)
                dve_softplus(nc, dve, low_done, 5 * g + HID[k] + 1, m.pm[k % 2][:, 0:B], buf, bias
                             ).then_inc(mm_read, 1)

            def step(g, par):
                dve.wait_ge(ids_in[par], nth(32, g, par))
                dd.dve_diag(dve, g, ids[par][:, 0:T])
                finish(g, 0, hid[:, :], m.b_b1)
                dd.dve_same(dve, g)
                finish(g, 1, dhid[par][0][:, :], m.b_ub1)
                finish(g, 2, dhid[par][1][:, :], m.b_ub1)
                finish(g, 3, dhid[par][2][:, :], m.b_ub1)
                dve.wait_ge(mm_done, K * g + 5)
                dve.wait_ge(dd.sum_mm, g)
                nc.vector.tensor_copy(msg[:, :, 0:D], m.pm[0][0:P, :].rearrange("p (t n) -> p t n", t=T)
                                      ).then_inc(mm_read, 1)
                finish(g, 5, dhid[par][3][:, :], m.b_ub1)
                dd.dve_lead(dve, g, par, lead_stored[par])
                for q in range(Q):
                    dve.wait_ge(mm_done, K * g + 7 + q)
                    nc.vector.bn_stats(m.stats[:, bass.ds(Q * g + q, 1), :].rearrange("p a b -> p (a b)"),
                                       m.pm[q % 2][:, 0:B]).then_inc(mm_read, 1)
            each_step(dve, step)


def nodes_mlp(nc, m, a):
    with ExitStack() as ctx:
        sb, sem, pool_sem = allocate(nc, m, ctx, "p1")
        ids = [sb(f"ids{i}", [P, 2 * T], I32) for i in range(2)]
        xs = [sb(f"xs{i}", [P, 2 * T, D]) for i in range(2)]
        ga = [sb(f"ga{i}", [P, 2 * T, AW]) for i in range(2)]
        deg = [sb(f"deg{i}", [P, 2 * T]) for i in range(2)]
        xT = [sb(f"xT{i}", [128, B]) for i in range(4)]
        h1 = [[sb(f"h1{i}{e}", [128, B]) for e in range(2)] for i in range(2)]
        h0 = sb("h0", [128, B])
        weight = sb("weight", [P, 2, T])
        us = [sb(f"us{i}", [P, T, D]) for i in range(2)]
        sq = [sb(f"sq{i}", [P, T, D]) for i in range(2)]
        ids_in = [sem(f"ids_in{i}") for i in range(2)]
        xs_in = [sem(f"xs_in{i}") for i in range(2)]
        ga_in = [pool_sem(f"ga_in{i}") for i in range(2)]
        h_stored = [sem(f"h_stored{i}") for i in range(2)]
        deg_stored = [sem(f"deg_stored{i}") for i in range(2)]
        cleared_next = sem("cleared_next")
        t_done, t_copied = sem("t_done"), sem("t_copied")
        mm_done, mm_read = sem("mm_done"), sem("mm_read")
        exp_done, ln_done, low_done = sem("exp_done"), sem("ln_done"), sem("low_done")
        deg_done, w_part, w_done = sem("deg_done"), sem("w_part"), sem("w_done")
        sq_done, corr_mm, corr_read = sem("sq_done"), sem("corr_mm"), sem("corr_read")
        sp_began, pool_began = sem("sp_began"), sem("pool_began")
        J, K = 4, 5
        src_v, dst_v = (a[k].rearrange("(p t) -> p t", p=P) for k in ("src", "dst"))
        zero_v = m.table[2][0:N, :].rearrange("(g p r) n -> g p (r n)", p=P, r=16)
        block = ctx.enter_context(nc.Block())

        @block.sync
        def _(sp):
            def until(signal, value):
                sp.wait_ge(signal, value)
                settled(sp, sp_began)

            def load(g, par):
                if not (isinstance(g, int) and g < 2):
                    until(ga_in[par], nth(128, g, par) - 128)
                    until(t_done, J * (g - 1))
                sp.dma_start(ids[par][:, 0:T], src_v[:, bass.ds(T * g, T)]).then_inc(ids_in[par], 16)
                sp.dma_start(ids[par][:, T:2 * T], dst_v[:, bass.ds(T * g, T)]).then_inc(ids_in[par], 16)
                sp.dma_start(xs[par][:, :, :].rearrange("p t n -> p (t n)"),
                             m.state[0][bass.ds(g, 1), :, :].rearrange("g p n -> (g p) n")).then_inc(xs_in[par], 16)

            def store(g, par):
                sp.dma_start(zero_v[bass.ds(g, 1), :, :].rearrange("g p n -> (g p) n"),
                             m.zero[0:P, :]).then_inc(cleared_next, 16)
                until(deg_done, g + 1)
                sp.dma_start(m.degree[bass.ds(g, 1), :, :].rearrange("g p n -> (g p) n"),
                             deg[par][:, :]).then_inc(deg_stored[par], 16)
                for e, k in ((0, 0), (1, 2)):
                    until(mm_read, K * g + k + 3)
                    sp.dma_start(m.slot_hidden[bass.ds(2 * g + e, 1), :, :].rearrange("g p n -> (g p) n"),
                                 h1[par][e][:, :]).then_inc(h_stored[par], 16)
            load(0, 0)
            load(1, 1)
            with sp.Fori(0, G - 3, 2) as g:
                store(g, 0)
                load(g + 2, 0)
                store(g + 1, 1)
                load(g + 3, 1)
            store(G - 3, 0)
            load(G - 1, 0)
            store(G - 2, 1)
            store(G - 1, 0)
            for par, n in ((0, (G + 1) // 2), (1, G // 2)):
                sp.wait_ge(h_stored[par], 32 * n)
                sp.wait_ge(deg_stored[par], 16 * n)
            sp.wait_ge(cleared_next, 16 * G)

        @block.gpsimd
        def _(pool):
            clear_spent(pool, m)

            def step(g, par):
                pool.wait_ge(ids_in[par], nth(32, g, par))
                if not (isinstance(g, int) and g < 2):
                    pool.wait_ge(t_done, J * (g - 1))
                    pool.wait_ge(deg_done, g - 1)
                settled(pool, pool_began)
                for k in range(2 * T):
                    pool.indirect_dma_start(out=ga[par][:, k, :], out_offset=None, in_=m.table[0][:, :],
                                            in_offset=index(ids[par][:, k:k + 1].bitcast(U32))).then_inc(ga_in[par], 16)
            each_step(pool, step)

        @block.tensor
        def _(pe):
            def turn(g, k, tiles):
                pe.wait_ge(t_copied, J * g + k + 1)
                for j in range(T):
                    last = nc.tensor.transpose(m.pt[k % 2][:, j * P:(j + 1) * P], tiles(j), m.ident[0:P, 0:P])
                last.then_inc(t_done, 1)

            def product(g, par, k):
                pe.wait_ge(mm_read, K * g + k + 1)
                return m.pm[(par * K + k) % 2]

            def step(g, par):
                pe.wait_ge(xs_in[par], nth(16, g, par))
                turn(g, 0, lambda j: xs[par][:, j, :])
                pe.wait_ge(ga_in[par], nth(128, g, par))
                turn(g, 1, lambda j: ga[par][:, j, 0:D])
                pe.wait_ge(t_copied, J * g + 1 + 3)
                bank = product(g, par, 0)
                nc.tensor.matmul(bank[:, 0:B], m.u1[:, 0, :], xT[0][:, :], start=True, stop=False)
                nc.tensor.matmul(bank[:, 0:B], m.u1[:, 1, :], xT[1][:, :], start=False, stop=True).then_inc(mm_done, 1)
                bank = product(g, par, 1)
                nc.tensor.matmul(bank[:, 0:B], m.u1[:, 0, :], xT[0][:, :], start=True, stop=True).then_inc(mm_done, 1)
                turn(g, 2, lambda j: xs[par][:, T + j, :])
                turn(g, 3, lambda j: ga[par][:, T + j, 0:D])
                pe.wait_ge(t_copied, J * g + 3 + 3)
                bank = product(g, par, 2)
                nc.tensor.matmul(bank[:, 0:B], m.u1[:, 0, :], xT[2][:, :], start=True, stop=False)
                nc.tensor.matmul(bank[:, 0:B], m.u1[:, 1, :], xT[3][:, :], start=False, stop=True).then_inc(mm_done, 1)
                for k, hid in ((3, h1[par][0]), (4, h0)):
                    pe.wait_ge(mm_read, K * g + (k - 3) + 3)
                    bank = product(g, par, k)
                    for j in range(T):
                        last = nc.tensor.matmul(bank[0:P, j * D:(j + 1) * D], hid[:, j * P:(j + 1) * P], m.u2[:, :],
                                                start=(j == 0), stop=(j == T - 1), skip_group_check=True)
                    last.then_inc(mm_done, 1)
                pe.wait_ge(mm_read, K * g + 4 + 3)
                pe.wait_ge(sq_done, 2 * (g + 1))
                pe.wait_ge(w_done, g + 1)
                pe.wait_ge(corr_read, 2 * g)
                for bank, x in ((m.pk, us), (m.pz, sq)):
                    for v in range(2):
                        for j in range(T):
                            last = nc.tensor.matmul(bank[:, 0:1], x[v][:, j, :], weight[:, v, j:j + 1],
                                                    start=(v + j == 0), stop=(v == 1 and j == T - 1))
                    last.then_inc(corr_mm, 1)
            each_step(pe, step)

        @block.scalar
        def _(act):
            nc.scalar.preload_act_table_set(TABLES)
            act.sem_inc(t_copied, 2)

            def copy(g, k):
                act.wait_ge(t_done, J * g + k + 1)
                act.wait_ge(mm_done, K * g)
                nc.scalar.copy(xT[k][:, :], m.pt[k % 2][:, 0:B]).then_inc(t_copied, 1)

            def softplus(g, par, k, buf):
                act.wait_ge(mm_done, K * g + k + 1)
                act_softplus(nc, act, exp_done, 3 * g + k + 1, m.pm[(par * K + k) % 2][:, 0:B], buf, m.b_ub1
                             ).then_inc(ln_done, 1)

            def step(g, par):
                copy(g, 0)
                copy(g, 1)
                act.wait_ge(h_stored[par], nth(32, g, par) - 32)
                softplus(g, par, 0, h1[par][0][:, :])
                softplus(g, par, 1, h0[:, :])
                copy(g, 2)
                copy(g, 3)
                softplus(g, par, 2, h1[par][1][:, :])
                act.wait_ge(corr_mm, 2 * g)
                for v in range(2):
                    act.wait_ge(mm_read, K * g + 3 + v + 3)
                    nc.scalar.square(sq[v][:, :, :], us[v][:, :, :]).then_inc(sq_done, 1)
            each_step(act, step)

        @block.vector
        def _(dve):
            dve.sem_inc(mm_read, 2)

            def finish(g, par, k, buf):
                dve.wait_ge(ln_done, 3 * g + k + 1)
                dve_softplus(nc, dve, low_done, 3 * g + k + 1, m.pm[(par * K + k) % 2][:, 0:B], buf, m.b_ub1
                             ).then_inc(mm_read, 1)

            def step(g, par):
                dve.wait_ge(ga_in[par], nth(128, g, par))
                dve.wait_ge(deg_stored[par], nth(16, g, par) - 16)
                nc.vector.tensor_copy(deg[par][:, :], ga[par][:, :, D]).then_inc(deg_done, 1)
                dve.wait_ge(corr_mm, 2 * g)
                nc.vector.tensor_scalar(weight[:, 1, :], ga[par][:, 0:T, D], 1.0, None, ALU.max).then_inc(w_part, 1)
                dve.wait_ge(w_part, 2 * g + 1)
                nc.vector.reciprocal(weight[:, 0, :], weight[:, 1, :]).then_inc(w_part, 1)
                dve.wait_ge(w_part, 2 * g + 2)
                nc.vector.tensor_scalar(weight[:, 1, :], weight[:, 0, :], -1.0, None, ALU.mult).then_inc(w_done, 1)
                finish(g, par, 0, h1[par][0][:, :])
                finish(g, par, 1, h0[:, :])
                finish(g, par, 2, h1[par][1][:, :])
                for v in range(2):
                    dve.wait_ge(mm_done, K * g + 4 + v)
                    nc.vector.tensor_copy(us[v][:, :, :], m.pm[(par * K + 3 + v) % 2][0:P, :].rearrange(
                        "p (t n) -> p t n", t=T)).then_inc(mm_read, 1)
                dve.wait_ge(corr_mm, 2 * (g + 1))
                for i, bank in enumerate((m.pk, m.pz)):
                    nc.vector.tensor_tensor(m.corr[:, i:i + 1], m.corr[:, i:i + 1], bank[:, 0:1], ALU.add
                                            ).then_inc(corr_read, 1)
                dve.wait_ge(corr_read, 2 * (g + 1))
            each_step(dve, step)


def batch_norm(nc, m):
    with ExitStack() as ctx:
        sb, sem, pool_sem = allocate(nc, m, ctx, "bn")
        v = sb("v", [128, 12])
        diag = sb("diag", [128, 2, D])
        row = sb("row", [128, D])
        tmp_b = sb("tmp_b", [128, 2 * D], BF16)
        tmp_f = sb("tmp_f", [128, 2 * D])
        chain, var_done, log_done, std_done = sem("chain"), sem("var_done"), sem("log_done"), sem("std_done")
        diag_done, spread = sem("diag_done"), sem("spread")
        block = ctx.enter_context(nc.Block())
        c = {name: v[:, i:i + 1] for i, name in enumerate(
            ("mean", "var", "c1", "c2", "sq", "log", "rstd", "scale", "bias", "mu"))}

        @block.vector
        def _(dve):
            n = 0

            def link(ins):
                nonlocal n
                n += 1
                ins.then_inc(chain, 1)
                dve.wait_ge(chain, n)

            def tt(o, x, y, op):
                link(nc.vector.tensor_tensor(c[o], c[x], c[y], op))
            link(nc.vector.bn_aggr(v[:, 0:2], m.stats[:, :, :].rearrange("p a b -> p (a b)")))
            link(nc.vector.tensor_scalar(v[:, 2:4], m.corr[:, :], 1.0 / N, None, ALU.mult))
            tt("sq", "mean", "mean", ALU.mult)
            tt("var", "var", "sq", ALU.add)
            tt("var", "var", "c2", ALU.add)
            tt("mean", "mean", "c1", ALU.add)
            tt("sq", "mean", "mean", ALU.mult)
            link(nc.vector.tensor_tensor(c["var"], c["var"], c["sq"], ALU.subtract))
            link(nc.vector.tensor_scalar(c["var"], c["var"], 0.0, None, ALU.max))
            dve.sem_inc(var_done, 1)
            dve.wait_ge(std_done, 1)
            tt("scale", "rstd", "rstd", ALU.max)
            link(nc.vector.tensor_tensor(c["scale"], c["rstd"], m.gamma, ALU.mult))
            link(nc.vector.tensor_tensor(c["mu"], c["mean"], m.ub2, ALU.add))
            link(nc.vector.tensor_tensor(c["bias"], m.ub2, c["mu"], ALU.subtract))
            tt("bias", "bias", "scale", ALU.mult)
            link(nc.vector.tensor_tensor(c["bias"], c["bias"], m.beta, ALU.add))
            link(nc.vector.tensor_scalar(diag[:, 0, :], m.ident[:, :], c["scale"], None, ALU.mult))
            nc.vector.tensor_scalar(diag[:, 1, :], m.ident[:, :], c["bias"], None, ALU.mult).then_inc(diag_done, 1)
            dve.wait_ge(spread, 1)
            link(nc.vector.tensor_tensor(m.u2s[:, :], m.u2[:, :], m.pm[0][:, 0:D], ALU.mult))
            link(nc.vector.tensor_copy(row[:, :], m.pm[0][:, D:2 * D]))
            split_row(nc, dve, link, m, row[:, :], m.l0row, tmp_b, tmp_f)

        @block.scalar
        def _(act):
            nc.scalar.preload_act_table_set(TABLES)
            act.wait_ge(var_done, 1)
            nc.scalar.activation(c["log"], c["var"], ACT.Ln, bias=m.eps[:, :]).then_inc(log_done, 1)
            act.wait_ge(log_done, 1)
            nc.scalar.activation(c["rstd"], c["log"], ACT.Exp, scale=-0.5).then_inc(std_done, 1)

        @block.tensor
        def _(pe):
            pe.wait_ge(diag_done, 1)
            nc.tensor.matmul(m.pm[0][:, 0:2 * D], m.ones[:, :], diag[:, :, :].rearrange("p a b -> p (a b)"),
                             start=True, stop=True).then_inc(spread, 1)


def dense_plan(phase):
    return {1: [(0, 0, False), (1, 1, False)], 2: [(2, 0, True)], 3: [(3, 1, True)], 4: []}[phase]


def layers(nc, m, a, phase, out):
    plan = dense_plan(phase)
    S = len(plan)
    with ExitStack() as ctx:
        sb, sem, pool_sem = allocate(nc, m, ctx, f"l{phase}")
        ends = [("end", e) for e in range(2)]
        nodes = [("node", s, l) for s in range(S) for l in (3, 2, 1, 0)]
        if S == 2:
            units = [ends[0]] + nodes[0:4] + [ends[1]] + nodes[4:8]
        elif S == 1:
            units = ends + nodes
        else:
            units = ends
        U = len(units)

        def turns_of(u):
            if u[0] == "node":
                return [("x", u)] if u[2] else []
            return {1: [], 2: [("x", u), ("sum", u)], 3: [("x", u)], 4: [("emb", u)]}[phase]
        order, jobs = [], []
        late = {1: [], 2: [[("turn", ("msg", 0))]] + [[("rel", j, h)] for j in range(T) for h in range(2)],
                3: [[("turn", ("msg", 0)), ("turn", ("msg", 1))], [("z",)], [("logit",)], [("weigh",)]], 4: []}[phase]
        order += [("turn", t) for t in turns_of(units[0])]
        if phase < 4:
            order += [("key",)]
        for n, u in enumerate(units):
            if n + 1 < U:
                order += [("turn", t) for t in turns_of(units[n + 1])]
            order += [("y", u)]
            if n:
                order += [("norm", units[n - 1])]
            order += [("stat", u)]
            if n == 1 and phase < 4:
                order += [("same",)]
            if n >= 2:
                for _ in range(2 if phase == 2 else 1):
                    if late:
                        order += late.pop(0)
        order += [("norm", units[-1])]
        for piece in late:
            order += piece
        if phase < 4:
            order += [("sum",)]
        jobs = [t for kind, *t in order if kind == "turn"]
        jobs = [t[0] for t in jobs]
        prods = [p[1] if p[0] == "y" else p for p in order if p[0] in ("y", "rel", "z")]
        J, K = max(len(jobs), 1), len(prods)
        normed = [p[1] for p in order if p[0] == "norm"]

        ids = [sb(f"ids{i}", [P, 2 * T], I32) for i in range(2)]
        xs = [sb(f"xs{i}", [P, 2 * T, D]) for i in range(2)]
        xo = [sb(f"xo{i}", [P, 2 * T, D]) for i in range(2)]
        if phase > 1:
            ga = [sb(f"ga{i}", [P, 2 * T, AW]) for i in range(2)]
            factor = sb("factor", [P, 2, 2 * T])
        if phase in (2, 4):
            deg = [sb(f"deg{i}", [P, 2 * T]) for i in range(2)]
        if phase == 1:
            hs = [[sb(f"hs{i}{e}", [128, B]) for e in range(2)] for i in range(2)]
        if phase == 2:
            kinds = [sb(f"kinds{i}", [P, T], I32) for i in range(2)]
            kindf, kmask = sb("kindf", [P, T]), sb("kmask", [P, T, R])
            prod = [sb(f"prod{i}", [P, R, D]) for i in range(2)]
        if phase == 3:
            hid = sb("hid", [128, B])
            gate = sb("gate", [P, T])
        if phase == 4:
            emb = sb("emb", [P, 2 * T, D])
        xT = {t: sb(f"xT{i}", [128, B]) for i, t in enumerate(jobs)}
        if phase < 4:
            if phase > 1:
                msg = sb("msg", [P, T, AW])
            sums = [sb(f"sums{i}", [P, T, AW]) for i in range(2)]
        rows = [sb(f"rows{i}", [P, 2 * T], I32) for i in range(2)]
        st, mv = sb("st", [P, U, T, 6]), sb("mv", [P, U, T, 2])
        logv, rstd = sb("logv", [P, U, T]), sb("rstd", [P, U, T])
        width = D if phase == 1 else AW

        ids_in = [sem(f"ids_in{i}") for i in range(2)]
        xs_in = [sem(f"xs_in{i}") for i in range(2)]
        ga_in = [pool_sem(f"ga_in{i}") for i in range(2)] if phase > 1 else None
        x_stored = [sem(f"x_stored{i}") for i in range(2)]
        nx_in = [sem(f"nx_in{i}") for i in range(2)] if S else None
        n_stored = [sem(f"n_stored{i}") for i in range(2)] if S else None
        lead_stored = [sem(f"lead_stored{i}") for i in range(2)] if phase == 2 else None
        cleared_next = sem("cleared_next") if phase == 1 else None
        summed = pool_sem("summed")
        t_done, t_copied = sem("t_done"), sem("t_copied")
        mm_done, mm_read = sem("mm_done"), sem("mm_read")
        st_done, mv_done, log_done, rstd_done, x_done = (sem(x) for x in ("st_done", "mv_done", "log_done",
                                                                          "rstd_done", "x_done"))
        pre_part, pre_done, y_part = (sem(x) for x in ("pre_part", "pre_done", "y_part"))
        msg_done, msg_part = sem("msg_done"), sem("msg_part")
        logit_mm, gate_arg, gate_exp = sem("logit_mm"), sem("gate_arg"), sem("gate_exp")
        sp_began, pool_began, dve_began = sem("sp_began"), sem("pool_began"), sem("dve_began")
        dd = Dedupe(nc, m, sb, sem, lead=(phase == 2)) if phase < 4 else None

        src_v, dst_v, kind_v = (a[k].rearrange("(p t) -> p t", p=P) for k in ("src", "dst", "edge_type_8"))
        xq = a["x"].rearrange("(g p q r) n -> q g p (r n)", p=P, q=Q, r=T)
        oq = out.rearrange("(g p q r) n -> q g p (r n)", p=P, q=Q, r=T)
        zero_v = m.table[3][0:N, :].rearrange("(g p r) n -> g p (r n)", p=P, r=16)
        IDS = {1: 48, 2: 48, 3: 48, 4: 64}[phase]
        XS = {1: 48, 2: 32, 3: 16, 4: 32}[phase]

        def slot_par(s, par):
            _, first, flips = plan[s]
            return (first + par) % 2 if flips else first

        def x_of(u, par):
            if u[0] == "end":
                e = slice(T * u[1], T * (u[1] + 1))
                return xs[par][:, e, :], xo[par][:, e, :]
            p = slot_par(u[1], par)
            return m.xb[u[2]][p][:, :, :], m.xb[u[2] + 1][1 - p][:, :, :]

        def layer_of(u):
            return phase - 1 if u[0] == "end" else u[2]

        def count(seq, item, g):
            return len(seq) * g + seq.index(item) + 1

        def read(item, g):
            return (K * g + prods.index(item) if item in prods else J * g + jobs.index(item)) + 3

        def nodes_wait(eng, g, par, u):
            p = slot_par(u[1], par)
            if S == 2:
                eng.wait_ge(nx_in[p], 32 * (g + 1))
            else:
                eng.wait_ge(nx_in[p], nth(32, g, par))

        block = ctx.enter_context(nc.Block())

        @block.sync
        def _(sp):
            def until(signal, value):
                sp.wait_ge(signal, value)
                settled(sp, sp_began)

            def whole(t, g):
                return t[bass.ds(g, 1), :, :].rearrange("g p n -> (g p) n")

            def flat(t):
                return t.rearrange("p t n -> p (t n)")

            def load(g, par):
                if not (isinstance(g, int) and g < 2):
                    until(x_done, U * (g - 1))
                    if phase < 4:
                        until(dd.sum_mm, g - 1)
                        until(summed, 64 * (g - 1))
                    else:
                        until(summed, 128 * (g - 1))
                sp.dma_start(ids[par][:, 0:T], src_v[:, bass.ds(T * g, T)]).then_inc(ids_in[par], 16)
                sp.dma_start(ids[par][:, T:2 * T], dst_v[:, bass.ds(T * g, T)]).then_inc(ids_in[par], 16)
                if phase in (1, 3, 4):
                    sp.dma_start(rows[par][:, 0:T], whole(m.lead[0], g)).then_inc(ids_in[par], 16)
                if phase == 4:
                    sp.dma_start(rows[par][:, T:2 * T], whole(m.lead[1], g)).then_inc(ids_in[par], 16)
                if phase == 2:
                    sp.dma_start(kinds[par][:, :], kind_v[:, bass.ds(T * g, T)]).then_inc(ids_in[par], 16)
                sp.dma_start(flat(xs[par][:, :, :]), whole(m.state[phase - 1], g)).then_inc(xs_in[par], 16)
                if phase in (2, 4):
                    sp.dma_start(deg[par][:, :], whole(m.degree, g)).then_inc(xs_in[par], 16)
                if phase == 1:
                    for e in range(2):
                        sp.dma_start(hs[par][e][:, :], whole(m.slot_hidden, 2 * g + e)).then_inc(xs_in[par], 16)

            def load_nodes(g, s, par):
                q, p = plan[s][0], slot_par(s, par)
                sp.dma_start(flat(m.xb[0][p][:, :, :]), whole(xq[q], g)).then_inc(nx_in[p], 16)
                sp.dma_start(m.hb[p][:, :], whole(m.hidden, Q * g + q)).then_inc(nx_in[p], 16)

            def store_nodes(g, s, par):
                if phase == 1:
                    at = (g - 2, 1) if s == 0 else (g - 1, 0)
                elif isinstance(g, int) and g < 3:
                    at = {2: ((G - 2, 1), (G - 1, 0), (G - 1, 1)), 3: tuple((G - 3 + i, 2) for i in range(3))}[phase][g]
                else:
                    at = (g - 3, phase)
                until(x_done, count(normed, ("node", s, 3), g))
                if phase > 1 or not (isinstance(g, int) and (g < 1 or (g < 2 and s == 0))):
                    p = slot_par(s, par)
                    sp.dma_start(whole(oq[at[1]], at[0]), flat(m.xb[4][1 - p][:, :, :])).then_inc(n_stored[p], 16)
                else:
                    sp.sem_inc(n_stored[slot_par(s, par)], 16)

            def step(g, par, nodes_next, load_next):
                for s in range(S):
                    store_nodes(g, s, par)
                    if nodes_next is not None:
                        until(x_done, count(normed, ("node", s, 0), g))
                        load_nodes(g + nodes_next, s, par if nodes_next == 2 else 1 - par)
                if phase == 1:
                    sp.dma_start(whole(zero_v, g), m.zero[0:P, :]).then_inc(cleared_next, 16)
                until(x_done, U * (g + 1))
                if phase < 4:
                    sp.dma_start(whole(m.state[phase], g), flat(xo[par][:, :, :])).then_inc(x_stored[par], 16)
                if phase == 2:
                    until(dd.lidx_done, g + 1)
                    sp.dma_start(whole(m.lead[1], g), dd.lidx[par][:, :].bitcast(I32)).then_inc(lead_stored[par], 16)
                if load_next:
                    load(g + 2, par)
            ahead = 2 if S == 1 else 1
            load(0, 0)
            load(1, 1)
            for g in range(ahead if S else 0):
                for s in range(S):
                    load_nodes(g, s, g % 2)

            def one(g, par):
                nodes_next = ahead if S and g + ahead < G else None
                step(g, par, nodes_next, g + 2 < G)
            for g in range(4):
                one(g, g % 2)
            with sp.Fori(4, G - 3, 2) as g:
                step(g, 0, ahead if S else None, True)
                step(g + 1, 1, ahead if S else None, True)
            for g in range(G - 3, G):
                one(g, g % 2)
            for par, n in ((0, (G + 1) // 2), (1, G // 2)):
                if phase < 4:
                    sp.wait_ge(x_stored[par], 16 * n)
                if phase == 2:
                    sp.wait_ge(lead_stored[par], 16 * n)
            for p in range(2 if S else 0):
                sp.wait_ge(n_stored[p], 16 * sum(slot_par(s, g % 2) == p for g in range(G) for s in range(S)))
            if phase == 1:
                sp.wait_ge(cleared_next, 16 * G)

        @block.gpsimd
        def _(pool):
            clear_spent(pool, m)

            def gather(g, par, e):
                pool.wait_ge(ids_in[par], nth(IDS, g, par))
                if not (isinstance(g, int) and g < 2):
                    pool.wait_ge(x_done, U * (g - 1))
                settled(pool, pool_began)
                for k in range(T * e, T * e + T):
                    pool.indirect_dma_start(out=ga[par][:, k, :], out_offset=None, in_=m.table[phase - 1][:, :],
                                            in_offset=index(ids[par][:, k:k + 1].bitcast(U32))).then_inc(ga_in[par], 16)

            def scatter(g, par):
                pool.wait_ge(dd.sum_copied, 2 * (g + 1))
                if phase == 2:
                    pool.wait_ge(dd.lidx_done, g + 1)
                else:
                    pool.wait_ge(ids_in[par], nth(IDS, g, par))
                pool.wait_ge(summed, 64 * g)
                settled(pool, pool_began)
                for j in range(T):
                    at = dd.lidx[par][:, j:j + 1] if phase == 2 else rows[par][:, j:j + 1].bitcast(U32)
                    pool.indirect_dma_start(out=m.table[phase][:, :], out_offset=index(at), in_=sums[par][:, j, :],
                                            in_offset=None, compute_op=ALU.add).then_inc(summed, 16)

            def finals(g, par, e):
                pool.wait_ge(x_done, U * (g + 1))
                pool.wait_ge(summed, 128 * g + 64 * e)
                settled(pool, pool_began)
                for k in range(T * e, T * e + T):
                    pool.indirect_dma_start(out=out[:, :], out_offset=index(rows[par][:, k:k + 1].bitcast(U32)),
                                            in_=xo[par][:, k, :], in_offset=None, bounds_check=N - 1,
                                            oob_is_err=False).then_inc(summed, 16)

            def turn(g, par, first=False):
                if phase > 1:
                    gather(g, par, 0)
                if phase == 4 and not first:
                    finals(g - 1, 1 - par, 0)
                if phase > 1:
                    gather(g, par, 1)
                if first:
                    return
                if phase == 4:
                    finals(g - 1, 1 - par, 1)
                else:
                    scatter(g - 1, 1 - par)
            turn(0, 0, True)
            turn(1, 1)
            turn(2, 0)
            with pool.Fori(3, G, 2) as g:
                turn(g, 1)
                turn(g + 1, 0)
            if phase == 4:
                finals(G - 1, 0, 0)
                finals(G - 1, 0, 1)
                pool.wait_ge(summed, 128 * G)
            else:
                scatter(G - 1, 0)
                pool.wait_ge(summed, 64 * G)

        @block.tensor
        def _(pe):
            def turn(g, par, job):
                kind, u = job
                if kind == "msg":
                    pe.wait_ge(x_done, count(normed, ("end", u), g))
                    tiles = xo[par][:, T * u:T * (u + 1), :]
                elif kind == "sum":
                    pe.wait_ge(pre_done, g + 1)
                    tiles = ga[par][:, T * u[1]:T * (u[1] + 1), 0:D]
                elif kind == "emb":
                    pe.wait_ge(pre_done, g + 1)
                    tiles = emb[:, T * u[1]:T * (u[1] + 1), :]
                else:
                    if u[0] == "end":
                        pe.wait_ge(xs_in[par], nth(XS, g, par))
                    elif u[1] == 0:
                        pe.wait_ge(x_done, U * g)
                    else:
                        pe.wait_ge(x_done, count(normed, ("node", 0, u[2] - 1), g))
                    tiles = x_of(u, par)[0]
                pe.wait_ge(t_copied, J * g + jobs.index(job) + 1)
                bank = m.pt[(par * J + jobs.index(job)) % 2]
                for j in range(T):
                    last = nc.tensor.transpose(bank[:, j * P:(j + 1) * P], tiles[:, j, :], m.ident[0:P, 0:P])
                last.then_inc(t_done, 1)

            def product(g, par, item):
                pe.wait_ge(mm_read, K * g + prods.index(item) + 1)
                return m.pm[(par * K + prods.index(item)) % 2]

            def y(g, par, u):
                l = layer_of(u)
                if l == 0:
                    if u[0] == "end":
                        pe.wait_ge(xs_in[par], nth(XS, g, par))
                        lhs = hs[par][u[1]]
                    else:
                        nodes_wait(pe, g, par, u)
                        lhs = m.hb[slot_par(u[1], par)]
                    pairs = [(lhs, m.u2s[:, :])]
                else:
                    w = {1: m.l1w[:, 0, :], 2: m.l2w[:, :], 3: m.wl[:, :]}[l]
                    pairs = [(xT[t], m.l1w[:, 1, :] if t[0] == "sum" else w) for t in turns_of(u)]
                    pe.wait_ge(t_copied, read(turns_of(u)[-1], g))
                bank = product(g, par, u)
                row = (m.l0row, m.l1row, m.l2row, m.l3row)[l]
                nc.tensor.matmul(bank[0:P, :], m.ones3[:, 0:P], row[:, :], start=True, stop=False)
                for i, (lhs, w) in enumerate(pairs):
                    for j in range(T):
                        last = nc.tensor.matmul(bank[0:P, j * D:(j + 1) * D], lhs[:, j * P:(j + 1) * P], w,
                                                start=False, stop=(i == len(pairs) - 1 and j == T - 1))
                last.then_inc(mm_done, 1)

            def step(g, par):
                for kind, *arg in order:
                    if kind == "turn":
                        turn(g, par, arg[0])
                    elif kind == "y":
                        y(g, par, arg[0])
                    elif kind == "key":
                        dd.pe_krow(pe, g)
                    elif kind == "same" and phase == 2:
                        dd.pe_count(pe, g)
                    elif kind == "rel":
                        j, h = arg
                        pe.wait_ge(t_copied, read(("msg", 0), g))
                        bank = product(g, par, ("rel", j, h))
                        nc.tensor.matmul(bank[0:P, :], xT[("msg", 0)][:, j * P:(j + 1) * P],
                                         m.wrel[:, 4 * h:4 * h + 4, :].rearrange("p r n -> p (r n)"),
                                         start=True, stop=True).then_inc(mm_done, 1)
                    elif kind == "z":
                        pe.wait_ge(t_copied, read(("msg", 1), g))
                        bank = product(g, par, ("z",))
                        for e in range(2):
                            last = nc.tensor.matmul(bank[:, 0:B], m.v1[:, e, :], xT[("msg", e)][:, :], start=(e == 0),
                                                    stop=(e == 1))
                        last.then_inc(mm_done, 1)
                    elif kind == "logit":
                        pe.wait_ge(mm_read, read(("z",), g))
                        pe.wait_ge(gate_arg, g)
                        for j in range(T):
                            last = nc.tensor.matmul(m.pz[0:P, j:j + 1], hid[:, j * P:(j + 1) * P], m.v2[:, :],
                                                    start=True, stop=True)
                        last.then_inc(logit_mm, 1)
                    elif kind == "sum":
                        if phase == 1:
                            pe.wait_ge(x_done, count(normed, ("end", 1), g))
                            dd.pe_sum(pe, g, lambda j: xo[par][:, T + j, :], D)
                        else:
                            pe.wait_ge(msg_done, g + 1)
                            dd.pe_sum(pe, g, lambda j: msg[:, j, :], AW)
            each_step(pe, step)

        @block.scalar
        def _(act):
            nc.scalar.preload_act_table_set(TABLES)
            act.sem_inc(t_copied, 2)

            def step(g, par):
                for kind, *arg in order:
                    if kind == "turn":
                        k = jobs.index(arg[0])
                        act.wait_ge(t_done, J * g + k + 1)
                        act.wait_ge(mm_done, K * g)
                        nc.scalar.copy(xT[arg[0]][:, :], m.pt[(par * J + k) % 2][:, 0:B]).then_inc(t_copied, 1)
                    elif kind == "stat":
                        n = units.index(arg[0])
                        act.wait_ge(mv_done, U * g + n + 1)
                        nc.scalar.activation(logv[:, n, :], mv[:, n, :, 1], ACT.Ln, bias=m.eps[0:P, :]).then_inc(log_done, 1)
                        act.wait_ge(log_done, U * g + n + 1)
                        nc.scalar.activation(rstd[:, n, :], logv[:, n, :], ACT.Exp, scale=-0.5).then_inc(rstd_done, 1)
                    elif kind == "key":
                        dd.act_krow(act, g)
                    elif kind == "logit":
                        act.wait_ge(gate_arg, g + 1)
                        nc.scalar.activation(gate[:, :], gate[:, :], ACT.Exp, scale=-1.0).then_inc(gate_exp, 1)
                    elif kind == "sum":
                        if not (isinstance(g, int) and g < 2):
                            act.wait_ge(summed, 64 * (g - 1))
                        dd.act_sum(act, g, sums[par], width)
            if phase == 1:
                for i in range(2):
                    nc.scalar.copy(sums[i][:, :, D:AW], m.zero[0:P, 0:T * (AW - D)].rearrange("p (t n) -> p t n", t=T))
            each_step(act, step)

        @block.vector
        def _(dve):
            dve.sem_inc(mm_read, 2)
            if phase in (2, 3):
                nc.vector.memset(msg[:, :, D:AW], 0.0).then_inc(msg_part, 1)
                dve.wait_ge(msg_part, 1)
            if phase == 2:
                nc.vector.memset(msg[:, :, D:D + 1], 1.0).then_inc(msg_part, 1)
                dve.wait_ge(msg_part, 2)

            def tile(t, u, j):
                return t[:, T * u[1] + j, :]

            def prepare(g, par):
                if phase == 1:
                    return
                parts = {2: 2, 3: 1, 4: 4}[phase]
                n = parts * g

                def part(ins):
                    nonlocal n
                    n = n + 1
                    ins.then_inc(pre_part, 1)
                    dve.wait_ge(pre_part, n)
                dve.wait_ge(ga_in[par], nth(128, g, par))
                if phase in (2, 4):
                    dve.wait_ge(xs_in[par], nth(XS, g, par))
                f0, f1 = factor[:, 0, :], factor[:, 1, :]
                if phase == 2:
                    part(nc.vector.tensor_scalar(f0, deg[par][:, :], 1.0, None, ALU.max))
                    part(nc.vector.reciprocal(f0, f0))
                    for k in range(2 * T):
                        last = nc.vector.tensor_scalar(ga[par][:, k, 0:D], ga[par][:, k, 0:D], f0[:, k:k + 1], None,
                                                       ALU.mult)
                    last.then_inc(pre_done, 1)
                elif phase == 3:
                    part(nc.vector.tensor_scalar(f0, ga[par][:, :, D], 1.0, None, ALU.max))
                    nc.vector.reciprocal(f0, f0).then_inc(pre_done, 1)
                    dve.wait_ge(pre_done, g + 1)
                elif phase == 4:
                    part(nc.vector.tensor_scalar(f1, ga[par][:, :, D], 1e-9, None, ALU.add))
                    part(nc.vector.reciprocal(f1, f1))
                    part(nc.vector.tensor_scalar(f0, deg[par][:, :], 0.0, 0.5, ALU.is_gt, ALU.mult))
                    part(nc.vector.tensor_tensor(f1, f1, f0, ALU.mult))
                    nc.vector.tensor_scalar(f0, f0, -1.0, 1.0, ALU.mult, ALU.add).then_inc(y_part, 1)
                    dve.wait_ge(y_part, 2 * g + 1)
                    dve.wait_ge(t_done, J * g)
                    for k in range(2 * T):
                        last = nc.vector.tensor_scalar(emb[:, k, :], xs[par][:, k, :], f0[:, k:k + 1], None, ALU.mult)
                    last.then_inc(y_part, 1)
                    dve.wait_ge(y_part, 2 * g + 2)
                    for k in range(2 * T):
                        last = nc.vector.scalar_tensor_tensor(emb[:, k, :], ga[par][:, k, 0:D], f1[:, k:k + 1],
                                                              emb[:, k, :], ALU.mult, ALU.add)
                    last.then_inc(pre_done, 1)

            def y(g, par, u):
                l = layer_of(u)
                x, o = x_of(u, par)
                bank = m.pm[(par * K + prods.index(u)) % 2][0:P, :].rearrange("p (t n) -> p t n", t=T)
                dve.wait_ge(mm_done, count(prods, u, g))
                if u[0] == "end":
                    dve.wait_ge(xs_in[par], nth(XS, g, par))
                    dve.wait_ge(x_stored[par], nth(16, g, par) - 16) if phase < 4 else None
                    if phase == 4 and not (isinstance(g, int) and g < 2):
                        dve.wait_ge(summed, 128 * (g - 1))
                else:
                    if u[2] == 0:
                        nodes_wait(dve, g, par, u)
                    if u[2] == 3:
                        if S == 2:
                            dve.wait_ge(n_stored[slot_par(u[1], par)], 16 * g)
                        else:
                            dve.wait_ge(n_stored[slot_par(u[1], par)], nth(16, g, par) - 16)
                    else:
                        if u[1] == 0:
                            dve.wait_ge(t_done, J * g)
                        else:
                            dve.wait_ge(t_done, count(jobs, ("x", ("node", 0, u[2] + 1)), g))
                if l < 2:
                    nc.vector.tensor_tensor(o, bank, x, ALU.add).then_inc(mm_read, 1)
                else:
                    if l == 2 and u[0] == "end":
                        for j in range(T):
                            last = nc.vector.scalar_tensor_tensor(bank[:, j, :], tile(ga[par], u, j)[:, 0:D],
                                                                  factor[:, 0, T * u[1] + j:T * u[1] + j + 1],
                                                                  bank[:, j, :], ALU.mult, ALU.add)
                        last.then_inc(y_part, 1)
                        dve.wait_ge(y_part, 2 * g + u[1] + 1)
                    nc.vector.scalar_tensor_tensor(o, bank, 0.0, x, ALU.max, ALU.add).then_inc(mm_read, 1)

            def step(g, par):
                for kind, *arg in order:
                    if kind == "key":
                        dve.wait_ge(ids_in[par], nth(IDS, g, par))
                        dd.dve_diag(dve, g, ids[par][:, T:2 * T] if phase == 2 else ids[par][:, 0:T])
                        if phase == 2:
                            nc.vector.tensor_copy(kindf[:, :], kinds[par][:, :]).then_inc(msg_part, 1)
                            dve.wait_ge(msg_part, 5 * g + 3)
                            nc.vector.tensor_tensor(kmask[:, :, :], kindf[:, :].unsqueeze(2).to_broadcast([P, T, R]),
                                                    m.relation[:, :].unsqueeze(1).to_broadcast([P, T, R]),
                                                    ALU.is_equal).then_inc(msg_part, 1)
                            dve.wait_ge(msg_part, 5 * g + 4)
                    elif kind == "same":
                        dd.dve_same(dve, g)
                        if phase == 2:
                            dd.dve_lead(dve, g, par, lead_stored[par])
                    elif kind == "y":
                        y(g, par, arg[0])
                    elif kind == "stat":
                        u, n = arg[0], units.index(arg[0])
                        o = x_of(u, par)[1]
                        dve.wait_ge(mm_read, read(u, g))
                        for j in range(T):
                            last = nc.vector.bn_stats(st[:, n, j, :], o[:, j, :])
                        last.then_inc(st_done, 1)
                        dve.wait_ge(st_done, U * g + n + 1)
                        settled(dve, dve_began)
                        for j in range(T):
                            last = nc.vector.bn_aggr(mv[:, n, j, :], st[:, n, j, :])
                        last.then_inc(mv_done, 1)
                    elif kind == "norm":
                        u, n = arg[0], units.index(arg[0])
                        o = x_of(u, par)[1]
                        dve.wait_ge(rstd_done, U * g + n + 1)
                        for j in range(T):
                            last = nc.vector.tensor_scalar(o[:, j, :], o[:, j, :], mv[:, n, j, 0:1],
                                                           rstd[:, n, j:j + 1], ALU.subtract, ALU.mult)
                        last.then_inc(x_done, 1)
                    elif kind == "rel":
                        j, h = arg
                        item = ("rel", j, h)
                        bank = m.pm[(par * K + prods.index(item)) % 2][0:P, :].rearrange("p (r n) -> p r n", r=4)
                        dve.wait_ge(mm_done, count(prods, item, g))
                        if h == 0:
                            if j == 1:
                                dve.wait_ge(msg_done, g)
                            else:
                                dve.wait_ge(msg_part, 5 * g + (5 if j == 2 else 6 if j == 3 else 2))
                        nc.vector.tensor_tensor(prod[j % 2][:, 4 * h:4 * h + 4, :], bank,
                                                kmask[:, j, 4 * h:4 * h + 4].unsqueeze(2).to_broadcast([P, 4, D]),
                                                ALU.mult).then_inc(mm_read, 1)
                        if h == 1:
                            dve.wait_ge(mm_read, read(item, g))
                            if j == 0:
                                dve.wait_ge(dd.sum_mm, g)
                            ins = nc.vector.tensor_reduce(msg[:, j, 0:D], prod[j % 2][:, :, :].rearrange("p r n -> p n r"),
                                                          mybir.AxisListType.X, ALU.add)
                            ins.then_inc(msg_done if j == T - 1 else msg_part, 1)
                    elif kind == "z":
                        bank = m.pm[(par * K + prods.index(("z",))) % 2][:, 0:B]
                        dve.wait_ge(mm_done, count(prods, ("z",), g))
                        dve.wait_ge(logit_mm, g)
                        nc.vector.tensor_scalar(hid[:, :], bank, m.b_v1, 0.0, ALU.add, ALU.max).then_inc(mm_read, 1)
                    elif kind == "logit":
                        dve.wait_ge(logit_mm, g + 1)
                        nc.vector.tensor_scalar(gate[:, :], m.pz[0:P, 0:T], m.nb2[0:P, :], -80.0, ALU.subtract,
                                                ALU.max).then_inc(gate_arg, 1)
                    elif kind == "weigh":
                        dve.wait_ge(gate_exp, g + 1)
                        dve.wait_ge(dd.sum_mm, g)
                        nc.vector.tensor_scalar(gate[:, :], gate[:, :], 1.0, None, ALU.add).then_inc(msg_part, 1)
                        dve.wait_ge(msg_part, 2 * g + 2)
                        nc.vector.reciprocal(gate[:, :], gate[:, :]).then_inc(msg_part, 1)
                        dve.wait_ge(msg_part, 2 * g + 3)
                        nc.vector.tensor_copy(msg[:, :, D], gate[:, :])
                        dve.wait_ge(x_done, count(normed, ("end", 1), g))
                        for j in range(T):
                            last = nc.vector.tensor_scalar(msg[:, j, 0:D], xo[par][:, T + j, :], gate[:, j:j + 1], None,
                                                           ALU.mult)
                        last.then_inc(msg_done, 1)
                if phase == 4:
                    return

            def whole_step(g, par):
                prepare(g, par)
                step(g, par)
            each_step(dve, whole_step)


def drain(nc, m, out):
    with ExitStack() as ctx:
        sb, sem, pool_sem = allocate(nc, m, ctx, "dr")
        units = [(t, l) for t in range(3) for l in range(3, t, -1)]
        xT = [sb(f"xT{i}", [128, B]) for i in range(len(units))]
        st, mv = sb("st", [P, T, 6]), sb("mv", [P, T, 2])
        logv, rstd = sb("logv", [P, T]), sb("rstd", [P, T])
        t_done, t_copied, mm_done, y_done = sem("t_done"), sem("t_copied"), sem("mm_done"), sem("y_done")
        st_done, mv_done, log_done, rstd_done, x_done = (sem(x) for x in ("st_done", "mv_done", "log_done",
                                                                          "rstd_done", "x_done"))
        stored = sem("stored")
        oq = out.rearrange("(g p q r) n -> q g p (r n)", p=P, q=Q, r=T)
        block = ctx.enter_context(nc.Block())

        def x_of(t, l):
            return m.xb[l][t % 2], m.xb[l + 1][1 - t % 2]

        @block.sync
        def _(sp):
            for n, (t, l) in enumerate(units):
                if l == 3:
                    sp.wait_ge(x_done, n + 1)
                    sp.dma_start(oq[Q - 1, G - 3 + t], x_of(t, l)[1][:, :, :].rearrange("p t n -> p (t n)")
                                 ).then_inc(stored, 16)
            sp.wait_ge(stored, 48)

        @block.tensor
        def _(pe):
            for n, (t, l) in enumerate(units):
                bank = m.pt[n % 2]
                if n:
                    pe.wait_ge(x_done, n)
                for j in range(T):
                    last = nc.tensor.transpose(bank[:, j * P:(j + 1) * P], x_of(t, l)[0][:, j, :], m.ident[0:P, 0:P])
                last.then_inc(t_done, 1)
                pe.wait_ge(t_copied, n + 1)
                row, w = {1: (m.l1row, m.l1w[:, 0, :]), 2: (m.l2row, m.l2w[:, :]), 3: (m.l3row, m.wl[:, :])}[l]
                bank = m.pm[n % 2]
                nc.tensor.matmul(bank[0:P, :], m.ones3[:, 0:P], row[:, :], start=True, stop=False)
                for j in range(T):
                    last = nc.tensor.matmul(bank[0:P, j * D:(j + 1) * D], xT[n][:, j * P:(j + 1) * P], w, start=False,
                                            stop=(j == T - 1))
                last.then_inc(mm_done, 1)

        @block.scalar
        def _(act):
            nc.scalar.preload_act_table_set(TABLES)
            for n, (t, l) in enumerate(units):
                act.wait_ge(t_done, n + 1)
                nc.scalar.copy(xT[n][:, :], m.pt[n % 2][:, 0:B]).then_inc(t_copied, 1)
                act.wait_ge(mv_done, n + 1)
                nc.scalar.activation(logv[:, :], mv[:, :, 1], ACT.Ln, bias=m.eps[0:P, :]).then_inc(log_done, 1)
                act.wait_ge(log_done, n + 1)
                nc.scalar.activation(rstd[:, :], logv[:, :], ACT.Exp, scale=-0.5).then_inc(rstd_done, 1)

        @block.vector
        def _(dve):
            for n, (t, l) in enumerate(units):
                x, o = x_of(t, l)
                bank = m.pm[n % 2][0:P, :].rearrange("p (t n) -> p t n", t=T)
                dve.wait_ge(mm_done, n + 1)
                if l == 3 and t == 2:
                    dve.wait_ge(stored, 48 - 16)
                if l == 1:
                    nc.vector.tensor_tensor(o[:, :, :], bank, x[:, :, :], ALU.add).then_inc(y_done, 1)
                else:
                    nc.vector.scalar_tensor_tensor(o[:, :, :], bank, 0.0, x[:, :, :], ALU.max, ALU.add
                                                   ).then_inc(y_done, 1)
                dve.wait_ge(y_done, n + 1)
                for j in range(T):
                    last = nc.vector.bn_stats(st[:, j, :], o[:, j, :])
                last.then_inc(st_done, 1)
                dve.wait_ge(st_done, n + 1)
                for j in range(T):
                    last = nc.vector.bn_aggr(mv[:, j, :], st[:, j, :])
                last.then_inc(mv_done, 1)
                dve.wait_ge(rstd_done, n + 1)
                for j in range(T):
                    last = nc.vector.tensor_scalar(o[:, j, :], o[:, j, :], mv[:, j, 0:1], rstd[:, j:j + 1],
                                                   ALU.subtract, ALU.mult)
                last.then_inc(x_done, 1)
                dve.wait_ge(x_done, n + 1)


def program(nc, a, out):
    m = Store()
    m.spent, m.fresh = [], []
    m.columns = ("L0_gnn_b1", "L0_gnn_ub1", "L3_gnn_b1", "L0_gnn_gamma", "L0_gnn_beta", "L0_gnn_ub2")
    with ExitStack() as ctx:
        m.ctx = ctx
        sb, sem, pool_sem = allocate(nc, m, ctx, "all")
        m.ident, m.ones = sb("ident", [128, D]), sb("ones", [128, D])
        m.ones3 = sb("ones3", [128, D], BF16)
        m.before = sb("before", [P, P])
        m.w1, m.w2 = sb("w1", [128, 3, D]), sb("w2", [128, D])
        m.u1, m.u2, m.u2s = sb("u1", [128, 2, D]), sb("u2", [128, D]), sb("u2s", [128, D])
        m.l1w, m.l2w = sb("l1w", [128, 2, D]), sb("l2w", [128, D])
        m.wrel, m.v1, m.v2, m.wl = sb("wrel", [128, R, D]), sb("v1", [128, 2, D]), sb("v2", [128, 1]), sb("wl", [128, D])
        m.col = sb("col", [128, len(m.columns)])
        m.b_b1, m.b_ub1, m.b_v1, m.gamma, m.beta, m.ub2 = (m.col[:, i:i + 1] for i in range(6))
        m.nb2, m.eps = sb("nb2", [128, 1]), sb("eps", [128, 1])
        m.b2row, m.l0row, m.l1row, m.l2row, m.l3row = (sb(f"row{i}", [128, T * D], BF16) for i in range(5))
        m.corr = sb("corr", [128, 2])
        m.relation = sb("relation", [P, R])
        m.hb = [sb(f"hb{i}", [128, B]) for i in range(2)]
        m.xb = [[sb(f"xb{l}{i}", [P, T, D]) for i in range(2)] for l in range(5)]
        m.sink = sb("sink", [P, T])
        m.zero = sb("zero", [128, 16 * AW])
        m.stats = sb("stats", [128, Q * G, 6])
        m.pt = [ctx.enter_context(nc.psum_tensor(f"pt{i}", [128, 512], F32)) for i in range(2)]
        m.pm = [ctx.enter_context(nc.psum_tensor(f"pm{i}", [128, 512], F32)) for i in range(2)]
        m.pa = [ctx.enter_context(nc.psum_tensor(f"pa{i}", [128, 512], F32)) for i in range(2)]
        m.pk = ctx.enter_context(nc.psum_tensor("pk", [128, 512], F32))
        m.pz = ctx.enter_context(nc.psum_tensor("pz", [128, 512], F32))

        KIND = DEBUG_KIND
        def dram(name, shape, dt=F32):
            return nc.dram_tensor(name, shape, dt, kind=KIND).ap()
        m.table = [dram(f"table{i}", (N + SINK, AW)) for i in range(4)]
        m.state = [dram(f"state{i}", (G, P, 2 * T * D)) for i in range(4)]
        m.hidden = dram("hidden", (Q * G, 128, B))
        m.slot_hidden = dram("slot_hidden", (2 * G, 128, B))
        m.lead = [dram(f"lead{i}", (G, P, T), I32) for i in range(2)]
        m.degree = dram("degree", (G, P, 2 * T))
        setup(nc, m, a)
        edges_mlp(nc, m, a)
        nodes_mlp(nc, m, a)
        batch_norm(nc, m)
        for phase in (1, 2, 3):
            layers(nc, m, a, phase, out)
        drain(nc, m, out)
        layers(nc, m, a, 4, out)

DEBUG_KIND = "Internal"

_INS = ['x', 'src', 'dst', 'edge_attr_128', 'edge_type_8', 'L0_gnn_W1', 'L0_gnn_b1', 'L0_gnn_W2', 'L0_gnn_b2',
        'L0_gnn_U1', 'L0_gnn_ub1', 'L0_gnn_U2', 'L0_gnn_ub2', 'L0_gnn_gamma', 'L0_gnn_beta', 'L1_gnn_W', 'L1_gnn_b',
        'L2_gnn_W_rel', 'L2_gnn_W_self_w', 'L2_gnn_W_self_b', 'L3_gnn_W1', 'L3_gnn_b1', 'L3_gnn_W2', 'L3_gnn_b2',
        'L3_gnn_Wl', 'L3_gnn_bl']


def kernel(**inputs):
    import numpy as _np
    import concourse.bacc as _bacc
    from concourse import mybir as _mybir
    from concourse.bass_utils import run_bass_kernel_spmd as _run

    nc = _bacc.Bacc("TRN2", target_bir_lowering=False, num_devices=1)
    arrays, args = {}, {}
    for name in _INS:
        arr = _np.ascontiguousarray(inputs[name])
        arrays[f"in_{name}"] = arr
        args[name] = nc.dram_tensor(f"in_{name}", arr.shape, _mybir.dt.from_np(arr.dtype), kind="ExternalInput").ap()
    out = nc.dram_tensor("out_0", (N, D), _mybir.dt.float32, kind="ExternalOutput").ap()
    program(nc, args, out)
    r = _run(nc, [arrays], core_ids=[0])
    return r.results[0]["out_0"]
```

```python
import concourse.bass as bass
from concourse import mybir
from contextlib import ExitStack

F32, BF16, I32, U32 = mybir.dt.float32, mybir.dt.bfloat16, mybir.dt.int32, mybir.dt.uint32
ALU = mybir.AluOpType
ACT = mybir.ActivationFunctionType

N, E, D, R = 50000, 12500, 128, 8
P, T = 125, 4
B = P * T
G = E // B
AW = 132
SINK = B
EPS = 1e-5
TABLES = "natural_log_exp_and_others"
Q = N // G // B


def nth(amount, g, par):
    return (g - par) * (amount // 2) + amount


def each_step(eng, step, n=G):
    step(0, 0)
    step(1, 1)
    with eng.Fori(2, n - 1, 2) as g:
        step(g, 0)
        step(g + 1, 1)
    step(n - 1, 0)


class Banks:

    def __init__(self, m, products, read):
        self.m, self.K, self.read = m, products, read
        self.of = [k % 3 for k in range(products)]
        if products % 3 == 1 and products > 1:
            self.of[-1] = 1

    def bank(self, k):
        return self.m.pm[self.of[k]]

    def free(self, eng, g, k):
        before = max(n for n in range(k - self.K, k) if self.of[n % self.K] == self.of[k])
        if not (isinstance(g, int) and self.K * g + before < 0):
            eng.wait_ge(self.read, self.K * g + before + 1)


def index(ap):
    return bass.IndirectOffsetOnAxis(ap=ap, axis=0)


def settled(eng, began):
    eng.sem_inc(began, 1)


class Store:
    pass


def allocate(nc, m, ctx, prefix):
    m.spent, m.fresh = m.spent + m.fresh, []

    def sb(name, shape, dt=F32):
        return ctx.enter_context(nc.sbuf_tensor(f"{prefix}_{name}", shape, dt))

    def sem(name):
        m.fresh.append(ctx.enter_context(nc.semaphore(f"{prefix}_{name}")))
        return m.fresh[-1]

    def pool_sem(name):
        return m.ctx.enter_context(nc.semaphore(f"{prefix}_{name}"))
    return sb, sem, pool_sem


def clear_spent(pool, m):
    for signal in m.spent:
        pool.sem_clear(signal)
    m.spent = []


def split_row(nc, dve, link, m, row, dst, tmp_b, tmp_f):
    link(nc.vector.tensor_copy(tmp_b[:, 0:D], row))
    link(nc.vector.tensor_tensor(tmp_f[:, 0:D], row, tmp_b[:, 0:D], ALU.subtract))
    link(nc.vector.tensor_copy(tmp_b[:, D:2 * D], tmp_f[:, 0:D]))
    link(nc.vector.tensor_tensor(tmp_f[:, D:2 * D], tmp_f[:, 0:D], tmp_b[:, D:2 * D], ALU.subtract))
    link(nc.vector.tensor_scalar(tmp_f[:, 0:D], tmp_b[:, 0:D], m.ident[:, 0:1], None, ALU.mult))
    link(nc.vector.scalar_tensor_tensor(tmp_f[:, 0:D], tmp_b[:, D:2 * D], m.ident[:, 1:2], tmp_f[:, 0:D],
                                        ALU.mult, ALU.add))
    link(nc.vector.scalar_tensor_tensor(tmp_f[:, 0:D], tmp_f[:, D:2 * D], m.ident[:, 2:3], tmp_f[:, 0:D],
                                        ALU.mult, ALU.add))
    for c in range(T):
        link(nc.vector.tensor_copy(dst[:, c * D:(c + 1) * D], tmp_f[:, 0:D]))


def setup(nc, m, a):
    with ExitStack() as ctx:
        sb, sem, pool_sem = allocate(nc, m, ctx, "setup")
        raw = sb("raw", [128, 3, D])
        tmp_b = sb("tmp_b", [128, 2 * D], BF16)
        tmp_f = sb("tmp_f", [128, 2 * D])
        rows = sb("rows", [128, 4, D])
        pat = sb("pat", [P, T], I32)
        pat8 = sb("pat8", [P, R], I32)
        loaded, raw_in, rows_in = sem("loaded"), sem("raw_in"), sem("rows_in")
        made, turned, chain = sem("made"), sem("turned"), sem("chain")
        n_loads = 0
        block = ctx.enter_context(nc.Block())

        @block.sync
        def _(sp):
            nonlocal n_loads
            sp.dma_start(raw[:, 0, :], a["L1_gnn_W"][:, 0:D]).then_inc(raw_in, 16)
            sp.dma_start(raw[:, 1, :], a["L1_gnn_W"][:, D:2 * D]).then_inc(raw_in, 16)
            sp.dma_start(raw[:, 2, :], a["L2_gnn_W_self_w"][:, :]).then_inc(raw_in, 16)
            for i, b in enumerate(("L0_gnn_b2", "L1_gnn_b", "L2_gnn_W_self_b", "L3_gnn_bl")):
                sp.dma_start(rows[:, i, :], a[b].partition_broadcast(128)).then_inc(rows_in, 16)
            for dst, src in (
                    (m.w1[:, :, :], a["L0_gnn_W1"].rearrange("(c p) n -> p c n", p=D)),
                    (m.w2[:, :], a["L0_gnn_W2"][:, :]),
                    (m.u1[:, :, :], a["L0_gnn_U1"].rearrange("(c p) n -> p c n", p=D)),
                    (m.u2[:, :], a["L0_gnn_U2"][:, :]),
                    (m.wrel[:, :, :], a["L2_gnn_W_rel"].rearrange("r p n -> p r n")),
                    (m.v1[:, :, :], a["L3_gnn_W1"].rearrange("(c p) n -> p c n", p=D)),
                    (m.v2[:, :], a["L3_gnn_W2"][:, :]),
                    (m.wl[:, :], a["L3_gnn_Wl"][:, :]),
                    (m.nb2[:, :], a["L3_gnn_b2"].partition_broadcast(128))):
                sp.dma_start(dst, src).then_inc(loaded, 16)
                n_loads += 1
            for i, b in enumerate(m.columns):
                sp.dma_start(m.col[:, i:i + 1], a[b].rearrange("(p n) -> p n", n=1)).then_inc(loaded, 16)
                n_loads += 1
            sp.wait_ge(loaded, 16 * n_loads)

        @block.gpsimd
        def _(pool):
            clear_spent(pool, m)

            nc.gpsimd.memset(m.ident[:, :], 0.0).then_inc(made, 1)
            nc.gpsimd.memset(m.before[:, :], 1.0).then_inc(made, 1)
            nc.gpsimd.memset(m.ones3[:, :], 0.0).then_inc(made, 1)
            nc.gpsimd.memset(m.ones[:, :], 1.0).then_inc(made, 1)
            nc.gpsimd.memset(m.onesb[:, :], 1.0).then_inc(made, 1)
            nc.gpsimd.iota(pat[:, :], pattern=[[P, T]], base=N, channel_multiplier=1).then_inc(made, 1)
            nc.gpsimd.iota(pat8[:, :], pattern=[[1, R]], base=0, channel_multiplier=0).then_inc(made, 1)
            pool.wait_ge(made, 7)
            nc.gpsimd.affine_select(out=m.ident[:, :], in_=m.ident[:, :], compare_op=ALU.not_equal, fill=1.0,
                                    base=0, pattern=[[-1, D]], channel_multiplier=1).then_inc(made, 1)
            nc.gpsimd.affine_select(out=m.before[:, :], in_=m.before[:, :], compare_op=ALU.is_gt, fill=0.0,
                                    base=0, pattern=[[1, P]], channel_multiplier=-1).then_inc(made, 1)
            nc.gpsimd.memset(m.ones3[0:3, :], 1.0).then_inc(made, 1)

        @block.vector
        def _(dve):
            n = 0

            def link(ins):
                nonlocal n
                n += 1
                ins.then_inc(chain, 1)
                dve.wait_ge(chain, n)
            link(nc.vector.memset(m.zero[:, :], 0.0))
            link(nc.vector.memset(m.eps[:, :], EPS))
            dve.wait_ge(made, 10)
            link(nc.vector.tensor_copy(m.sink[:, :], pat[:, :]))
            link(nc.vector.tensor_copy(m.relation[:, :], pat8[:, :]))
            link(nc.vector.memset(m.corr[:, :], 0.0))
            for l in range(1, 4):
                link(nc.vector.memset(m.xb[l][0][:, :, :], 0.0))
            dve.wait_ge(rows_in, 64)
            for i, dst in enumerate((m.b2row, m.l1row, m.l2row, m.l3row)):
                split_row(nc, dve, link, m, rows[:, i, :], dst, tmp_b, tmp_f)
            dve.wait_ge(loaded, 16 * n_loads)
            link(nc.vector.tensor_scalar(m.nb2[:, :], m.nb2[:, :], -1.0, None, ALU.mult))
            dve.wait_ge(turned, 3)
            link(nc.vector.tensor_copy(m.l1w[:, :, :], m.pm[0][:, 0:2 * D].rearrange("p (c n) -> p c n", c=2)))
            link(nc.vector.tensor_copy(m.l2w[:, :], m.pm[0][:, 2 * D:3 * D]))

        @block.tensor
        def _(pe):
            pe.wait_ge(raw_in, 48)
            pe.wait_ge(made, 10)
            for i in range(3):
                nc.tensor.transpose(m.pm[0][:, i * D:(i + 1) * D], raw[:, i, :], m.ident[:, :]).then_inc(turned, 1)


class Dedupe:

    def __init__(self, nc, m, sb, sem, lead, width):
        self.nc, self.m, self.lead, self.width = nc, m, lead, width
        self.krow = [sb(f"krow{i}", [P, B], I32) for i in range(2)]
        self.key = sb("key", [P, T])
        self.same = [sb(f"same{i}", [P, T, B], BF16) for i in range(2)]
        self.rest = [sb(f"rest{i}", [P, T, width]) for i in range(2)]
        self.key_done, self.same_done = sem("key_done"), sem("same_done")
        self.sum_mm, self.sum_copied = sem("sum_mm"), sem("sum_copied")
        self.split_part, self.split_done = sem("split_part"), sem("split_done")
        if lead:
            self.early = sb("early", [P, T, P], BF16)
            self.off = sb("off", [P, T])
            self.lidx = [sb(f"lidx{i}", [P, T], U32) for i in range(2)]
            self.early_done, self.cnt_mm = sem("early_done"), sem("cnt_mm")
            self.off_done, self.lidx_done = sem("off_done"), sem("lidx_done")

    def dve_same(self, dve, g, par, ids):
        nc, m = self.nc, self.m
        if self.lead:
            dve.wait_ge(self.lidx_done, g)
        dve.wait_ge(self.same_done, g)
        nc.vector.tensor_copy(self.key[:, :], ids).then_inc(self.key_done, 1)
        dve.wait_ge(self.key_done, g + 1)
        if not (isinstance(g, int) and g < 2):
            dve.wait_ge(self.sum_mm, g - 1)
        for j in range(T):
            last = nc.vector.tensor_scalar(self.same[par][:, j, :], self.krow[par][:, :], self.key[:, j:j + 1], None,
                                           ALU.is_equal)
        last.then_inc(self.same_done, 1)
        if self.lead:
            dve.wait_ge(self.same_done, g + 1)
            dve.wait_ge(self.cnt_mm, g)
            for j in range(T):
                last = nc.vector.tensor_tensor(self.early[:, j, :], self.same[par][:, j, j * P:(j + 1) * P],
                                               m.before[:, :], ALU.mult)
            last.then_inc(self.early_done, 1)

    def pe_count(self, pe, g, par):
        nc, m = self.nc, self.m
        pe.wait_ge(self.early_done, g + 1)
        pe.wait_ge(self.lidx_done, g)
        for i in range(T):
            for j in range(i + 1):
                lhs = self.early[:, i, :] if i == j else self.same[par][:, j, i * P:(i + 1) * P]
                last = nc.tensor.matmul(m.pz[0:P, i:i + 1], lhs, m.onesb[0:P, 0:1], start=(j == 0), stop=(j == i))
        last.then_inc(self.cnt_mm, 1)

    def dve_lead(self, dve, g, par, stored, summed):
        nc, m = self.nc, self.m
        dve.wait_ge(self.lidx_done, g)
        nc.vector.tensor_tensor(self.off[:, :], m.sink[:, :], self.key[:, :], ALU.subtract).then_inc(self.off_done, 1)
        dve.wait_ge(self.cnt_mm, g + 1)
        dve.wait_ge(self.off_done, 3 * g + 1)
        nc.vector.scalar_tensor_tensor(self.off[:, :], m.pz[0:P, 0:T], 0.5, self.off[:, :], ALU.is_gt,
                                       ALU.mult).then_inc(self.off_done, 1)
        dve.wait_ge(self.off_done, 3 * g + 2)
        nc.vector.tensor_tensor(self.off[:, :], self.off[:, :], self.key[:, :], ALU.add).then_inc(self.off_done, 1)
        dve.wait_ge(self.off_done, 3 * g + 3)
        dve.wait_ge(stored, nth(16, g, par) - 16)
        if not (isinstance(g, int) and g < 2):
            dve.wait_ge(summed, 64 * (g - 1))
        nc.vector.tensor_copy(self.lidx[par][:, :], self.off[:, :]).then_inc(self.lidx_done, 1)

    @staticmethod
    def upper(x):
        return x.bitcast(BF16).rearrange("p t (n h) -> p t n h", h=2)[:, :, :, 1]

    def pool_split(self, pool, g, msg):
        nc = self.nc
        pool.wait_ge(self.sum_mm, g)
        nc.gpsimd.tensor_tensor(self.rest[0][:, :, :], msg, self.upper(msg), ALU.subtract).then_inc(self.split_part, 1)
        pool.wait_ge(self.split_part, g + 1)
        nc.gpsimd.tensor_tensor(self.rest[1][:, :, :], self.rest[0][:, :, :], self.upper(self.rest[0][:, :, :]),
                                ALU.subtract).then_inc(self.split_done, 1)

    def pe_sum(self, pe, g, par, msg):
        nc, m, w = self.nc, self.m, self.width
        pe.wait_ge(self.same_done, g + 1)
        pe.wait_ge(self.split_done, g + 1)
        pe.wait_ge(self.sum_copied, 2 * g)
        parts = [self.upper(x) for x in (msg, self.rest[0][:, :, :], self.rest[1][:, :, :])]
        for i in range(T):
            for j in range(T):
                for n, x in enumerate(parts):
                    last = nc.tensor.matmul(m.pa[i // 2][0:P, (i % 2) * AW:(i % 2) * AW + w],
                                            self.same[par][:, j, i * P:(i + 1) * P], x[:, j, :],
                                            start=(j + n == 0), stop=(j == T - 1 and n == 2))
        last.then_inc(self.sum_mm, 1)

    def act_sum(self, act, g, dst):
        act.wait_ge(self.sum_mm, g + 1)
        for i in range(2):
            self.nc.scalar.copy(dst[:, 2 * i:2 * i + 2, 0:self.width],
                                self.m.pa[i][0:P, 0:2 * AW].rearrange("p (c n) -> p c n", c=2)[:, :, 0:self.width]
                                ).then_inc(self.sum_copied, 1)


def act_softplus(nc, act, exp_done, n, z, buf, bias):
    nc.scalar.activation(buf, z, ACT.Exp, bias=bias).then_inc(exp_done, 1)
    act.wait_ge(exp_done, n)
    return nc.scalar.activation(buf, buf, ACT.Ln, bias=1.0)


def dve_softplus(nc, dve, low_done, n, z, buf, bias):
    nc.vector.tensor_scalar(buf, buf, 40.0, None, ALU.min).then_inc(low_done, 1)
    dve.wait_ge(low_done, n)
    return nc.vector.scalar_tensor_tensor(buf, z, bias, buf, ALU.add, ALU.max)


def edges_mlp(nc, m, a):
    with ExitStack() as ctx:
        sb, sem, pool_sem = allocate(nc, m, ctx, "p0")
        ids = [sb(f"ids{i}", [P, 2 * T], I32) for i in range(2)]
        gx = [sb(f"gx{i}", [P, 2 * T, D]) for i in range(2)]
        ea = [sb(f"ea{i}", [P, T, D]) for i in range(2)]
        dx = [sb(f"dx{i}", [P, 4 * T, D]) for i in range(2)]
        xT = [sb(f"xT{i}", [128, B]) for i in range(7)]
        hid = sb("hid", [128, B])
        dhid = [[sb(f"dhid{i}{q}", [128, B]) for q in range(Q)] for i in range(2)]
        msg = sb("msg", [P, T, AW])
        out = [sb(f"out{i}", [P, T, AW]) for i in range(2)]
        ids_in = [sem(f"ids_in{i}") for i in range(2)]
        src_in = [pool_sem(f"src_in{i}") for i in range(2)]
        dst_in = [pool_sem(f"dst_in{i}") for i in range(2)]
        ea_in = [sem(f"ea_in{i}") for i in range(2)]
        dx_in = [sem(f"dx_in{i}") for i in range(2)]
        x_stored = [sem(f"x_stored{i}") for i in range(2)]
        h_stored = [sem(f"h_stored{i}") for i in range(2)]
        lead_stored = [sem(f"lead_stored{i}") for i in range(2)]
        cleared, cleared_next, summed = sem("cleared"), sem("cleared_next"), pool_sem("summed")
        t_done, t_copied = sem("t_done"), sem("t_copied")
        mm_done, mm_read = sem("mm_done"), sem("mm_read")
        exp_done, ln_done, low_done, prepared = sem("exp_done"), sem("ln_done"), sem("low_done"), sem("prepared")
        sp_began, pool_began = sem("sp_began"), sem("pool_began")
        dd = Dedupe(nc, m, sb, sem, lead=True, width=AW)
        J, K = 7, 10
        HID = {0: 0, 1: 1, 2: 2, 3: 3, 5: 4}
        NODE = {1: 0, 2: 1, 3: 2, 5: 3}
        banks = Banks(m, K, mm_read)
        src_v, dst_v = (a[k].rearrange("(g t p) -> g p t", t=T, p=P) for k in ("src", "dst"))
        ea_v = a["edge_attr_128"].rearrange("(g t p) n -> g p t n", t=T, p=P)
        x_v = a["x"].rearrange("(g p r) n -> g p (r n)", p=P, r=4 * T)
        zero_v = [t[0:N, :].rearrange("(g p r) n -> g p (r n)", p=P, r=16) for t in m.table]
        block = ctx.enter_context(nc.Block())

        @block.sync
        def _(sp):
            def until(signal, value):
                sp.wait_ge(signal, value)
                settled(sp, sp_began)

            def load(g, par):
                until(src_in[par], nth(64, g, par) - 64)
                until(dst_in[par], nth(64, g, par) - 64)
                if not (isinstance(g, int) and g < 2):
                    until(dd.same_done, g - 1)
                    until(t_done, J * (g - 1))
                sp.dma_start(ids[par][:, 0:T], src_v[bass.ds(g, 1), :, :].rearrange("g p t -> (g p) t"),
                             allow_slow_non_contiguous=True).then_inc(ids_in[par], 16)
                sp.dma_start(ids[par][:, T:2 * T], dst_v[bass.ds(g, 1), :, :].rearrange("g p t -> (g p) t"),
                             allow_slow_non_contiguous=True).then_inc(ids_in[par], 16)
                sp.dma_start(dd.krow[par][:, :], a["src"][bass.ds(B * g, B)].partition_broadcast(P)
                             ).then_inc(ids_in[par], 16)
                sp.dma_start(ea[par][:, :, :], ea_v[bass.ds(g, 1), :, :, :].rearrange("g p t n -> (g p) t n")).then_inc(ea_in[par], 16)
                for lo, hi in ((0, 112), (112, P)):
                    sp.dma_start(dx[par][lo:hi, :, :].rearrange("p r n -> p (r n)"),
                                 x_v[bass.ds(g, 1), lo:hi, :].rearrange("g p n -> (g p) n")).then_inc(dx_in[par], 16)

            def store(g, par, more=True):
                until(src_in[par], nth(64, g, par))
                until(dst_in[par], nth(64, g, par))
                sp.dma_start(m.state[0][bass.ds(g, 1), :, :].rearrange("g p n -> (g p) n"),
                             gx[par][:, :, :].rearrange("p t n -> p (t n)")).then_inc(x_stored[par], 16)
                sp.dma_start(zero_v[1][bass.ds(g, 1), :, :].rearrange("g p n -> (g p) n"),
                             m.zero[0:P, :]).then_inc(cleared_next, 16)
                for k, q in NODE.items():
                    if q == 3 and more:
                        load(g + 2, par)
                    until(mm_read, K * g + k + 1)
                    sp.dma_start(m.hidden[bass.ds(Q * g + q, 1), :, :].rearrange("g p n -> (g p) n"),
                                 dhid[par][q][:, :]).then_inc(h_stored[par], 16)
                until(dd.lidx_done, g + 1)
                sp.dma_start(m.lead[0][bass.ds(g, 1), :, :].rearrange("g p n -> (g p) n"),
                             dd.lidx[par][:, :].bitcast(I32)).then_inc(lead_stored[par], 16)
            load(0, 0)
            load(1, 1)
            for g in range(G):
                sp.dma_start(zero_v[0][g], m.zero[0:P, :]).then_inc(cleared, 16)
            for t in m.table:
                sp.dma_start(t[N:N + SINK, :].rearrange("(p r) n -> p (r n)", p=P),
                             m.zero[0:P, 0:T * AW]).then_inc(cleared, 16)
            with sp.Fori(0, G - 3, 2) as g:
                store(g, 0)
                store(g + 1, 1)
            store(G - 3, 0)
            store(G - 2, 1, False)
            store(G - 1, 0, False)
            for par, n in ((0, (G + 1) // 2), (1, G // 2)):
                sp.wait_ge(x_stored[par], 16 * n)
                sp.wait_ge(h_stored[par], 64 * n)
                sp.wait_ge(lead_stored[par], 16 * n)
            sp.wait_ge(cleared_next, 16 * G)

        @block.gpsimd
        def _(pool):
            clear_spent(pool, m)

            def gather(g, par):
                pool.wait_ge(ids_in[par], nth(48, g, par))
                pool.wait_ge(x_stored[par], nth(16, g, par) - 16)
                if not (isinstance(g, int) and g < 2):
                    pool.wait_ge(t_done, J * (g - 1))
                settled(pool, pool_began)
                for s, got in ((0, src_in), (1, dst_in)):
                    for j in range(T):
                        k = T * s + j
                        pool.indirect_dma_start(out=gx[par][:, k, :], out_offset=None, in_=a["x"][:, :],
                                                in_offset=index(ids[par][:, k:k + 1].bitcast(U32))
                                                ).then_inc(got[par], 16)

            def scatter(g, par):
                pool.wait_ge(dd.lidx_done, g + 1)
                pool.wait_ge(dd.sum_copied, 2 * (g + 1))
                pool.wait_ge(summed, 64 * g)
                settled(pool, pool_began)
                for j in range(T):
                    pool.indirect_dma_start(out=m.table[0][:, :], out_offset=index(dd.lidx[par][:, j:j + 1]),
                                            in_=out[par][:, j, :], in_offset=None, compute_op=ALU.add
                                            ).then_inc(summed, 16)
            def split(g):
                pool.wait_ge(mm_read, K * g + 4 + 1)
                dd.pool_split(pool, g, msg[:, :, :])

            def turn(g, par, more=True):
                split(g)
                if more:
                    gather(g + 2, par)
                scatter(g, par)

            gather(0, 0)
            gather(1, 1)
            pool.wait_ge(cleared, 16 * (G + 4))
            turn(0, 0)
            with pool.Fori(1, G - 2, 2) as g:
                turn(g, 1)
                turn(g + 1, 0)
            turn(G - 2, 1, False)
            turn(G - 1, 0, False)
            pool.wait_ge(summed, 64 * G)

        @block.tensor
        def _(pe):
            def turn(g, par, k, tiles):
                pe.wait_ge(t_copied, J * g + k + 1)
                bank = m.pt[(par * J + k) % 2]
                for j in range(T):
                    last = nc.tensor.transpose(bank[:, j * P:(j + 1) * P], tiles(j), m.ident[0:P, 0:P])
                last.then_inc(t_done, 1)

            def node_hidden(g, k):
                q = NODE[k]
                pe.wait_ge(t_copied, J * g + 3 + q + 3)
                banks.free(pe, g, k)
                nc.tensor.matmul(banks.bank(k)[:, 0:B], m.u1[:, 0, :], xT[3 + q][:, :], start=True,
                                 stop=True).then_inc(mm_done, 1)

            def node_output(g, par, q):
                k = [k for k in NODE if NODE[k] == q][0]
                pe.wait_ge(mm_read, K * g + k + 1)
                banks.free(pe, g, 6 + q)
                nc.tensor.matmul(banks.bank(6 + q)[:, 0:B], m.u2[:, :], dhid[par][q][:, :], start=True,
                                 stop=True).then_inc(mm_done, 1)

            def first_turns(g, par):
                pe.wait_ge(src_in[par], nth(64, g, par))
                turn(g, par, 0, lambda j: gx[par][:, j, :])
                pe.wait_ge(dst_in[par], nth(64, g, par))
                turn(g, par, 1, lambda j: gx[par][:, T + j, :])
                pe.wait_ge(ea_in[par], nth(16, g, par))
                turn(g, par, 2, lambda j: ea[par][:, j, :])
                pe.wait_ge(dx_in[par], nth(32, g, par))
                turn(g, par, 3, lambda j: dx[par][:, j, :])

            def step(g, par):
                pe.wait_ge(t_copied, J * g + 2 + 3)
                banks.free(pe, g, 0)
                for c in range(3):
                    last = nc.tensor.matmul(banks.bank(0)[:, 0:B], m.w1[:, c, :], xT[c][:, :], start=(c == 0),
                                            stop=(c == 2))
                last.then_inc(mm_done, 1)
                turn(g, par, 4, lambda j: dx[par][:, T + j, :])
                node_hidden(g, 1)
                turn(g, par, 5, lambda j: dx[par][:, 2 * T + j, :])
                node_hidden(g, 2)
                turn(g, par, 6, lambda j: dx[par][:, 3 * T + j, :])
                if not (isinstance(g, int) and g == 0):
                    dd.pe_sum(pe, g - 1, 1 - par, msg[:, :, :])
                node_hidden(g, 3)
                pe.wait_ge(mm_read, K * g + 0 + 1)
                banks.free(pe, g, 4)
                nc.tensor.matmul(banks.bank(4)[0:P, :], m.ones3[:, 0:P], m.b2row[:, :], start=True, stop=False)
                for j in range(T):
                    last = nc.tensor.matmul(banks.bank(4)[0:P, j * D:(j + 1) * D], hid[:, j * P:(j + 1) * P], m.w2[:, :],
                                            start=False, stop=(j == T - 1))
                last.then_inc(mm_done, 1)
                node_hidden(g, 5)
                if not (isinstance(g, int) and g == G - 1):
                    first_turns(g + 1, 1 - par)
                node_output(g, par, 0)
                node_output(g, par, 1)
                dd.pe_count(pe, g, par)
                node_output(g, par, 2)
                node_output(g, par, 3)
            first_turns(0, 0)
            each_step(pe, step)
            dd.pe_sum(pe, G - 1, 0, msg[:, :, :])

        @block.scalar
        def _(act):
            nc.scalar.preload_act_table_set(TABLES)
            act.sem_inc(t_copied, 2)

            def copy(g, par, k):
                act.wait_ge(t_done, J * g + k + 1)
                if not (isinstance(g, int) and g == 0):
                    used = 0 if k < 3 else [n for n in NODE if NODE[n] == k - 3][0]
                    act.wait_ge(mm_done, K * (g - 1) + used + 1)
                nc.scalar.copy(xT[k][:, :], m.pt[(par * J + k) % 2][:, 0:B]).then_inc(t_copied, 1)

            def softplus(g, k, buf, bias):
                act.wait_ge(mm_done, K * g + k + 1)
                act_softplus(nc, act, exp_done, 5 * g + HID[k] + 1, banks.bank(k)[:, 0:B], buf, bias
                             ).then_inc(ln_done, 1)

            def sums(g, par):
                if not (isinstance(g, int) and g < 2):
                    act.wait_ge(summed, 64 * (g - 1))
                dd.act_sum(act, g, out[par])

            def step(g, par):
                if not (isinstance(g, int) and g == 0):
                    act.wait_ge(mm_done, K * (g - 1) + 4 + 1)
                softplus(g, 0, hid[:, :], m.b_b1)
                act.wait_ge(h_stored[par], nth(64, g, par) - 64)
                copy(g, par, 4)
                softplus(g, 1, dhid[par][0][:, :], m.b_ub1)
                copy(g, par, 5)
                softplus(g, 2, dhid[par][1][:, :], m.b_ub1)
                copy(g, par, 6)
                if not (isinstance(g, int) and g == 0):
                    sums(g - 1, 1 - par)
                softplus(g, 3, dhid[par][2][:, :], m.b_ub1)
                softplus(g, 5, dhid[par][3][:, :], m.b_ub1)
                if not (isinstance(g, int) and g == G - 1):
                    for k in range(4):
                        copy(g + 1, 1 - par, k)
            for k in range(4):
                copy(0, 0, k)
            each_step(act, step)
            sums(G - 1, 0)

        @block.vector
        def _(dve):
            nc.vector.memset(msg[:, :, D:AW], 0.0).then_inc(prepared, 1)
            dve.wait_ge(prepared, 1)
            nc.vector.memset(msg[:, :, D:D + 1], 1.0).then_inc(prepared, 1)

            def finish(g, k, buf, bias):
                dve.wait_ge(ln_done, 5 * g + HID[k] + 1)
                dve_softplus(nc, dve, low_done, 5 * g + HID[k] + 1, banks.bank(k)[:, 0:B], buf, bias
                             ).then_inc(mm_read, 1)

            def step(g, par):
                finish(g, 0, hid[:, :], m.b_b1)
                finish(g, 1, dhid[par][0][:, :], m.b_ub1)
                finish(g, 2, dhid[par][1][:, :], m.b_ub1)
                finish(g, 3, dhid[par][2][:, :], m.b_ub1)
                dve.wait_ge(mm_done, K * g + 5)
                dve.wait_ge(dd.sum_mm, g)
                nc.vector.tensor_copy(msg[:, :, 0:D], banks.bank(4)[0:P, :].rearrange("p (t n) -> p t n", t=T)
                                      ).then_inc(mm_read, 1)
                dve.wait_ge(ids_in[par], nth(48, g, par))
                dd.dve_same(dve, g, par, ids[par][:, 0:T])
                finish(g, 5, dhid[par][3][:, :], m.b_ub1)
                for q in range(Q):
                    if q == 3:
                        dd.dve_lead(dve, g, par, lead_stored[par], summed)
                    dve.wait_ge(mm_done, K * g + 7 + q)
                    nc.vector.bn_stats(m.stats[:, bass.ds(Q * g + q, 1), :].rearrange("p a b -> p (a b)"),
                                       banks.bank(6 + q)[:, 0:B]).then_inc(mm_read, 1)
            each_step(dve, step)


def nodes_mlp(nc, m, a):
    with ExitStack() as ctx:
        sb, sem, pool_sem = allocate(nc, m, ctx, "p1")
        ids = [sb(f"ids{i}", [P, 2 * T], I32) for i in range(2)]
        xs = [sb(f"xs{i}", [P, 2 * T, D]) for i in range(2)]
        ga = [sb(f"ga{i}", [P, 2 * T, AW]) for i in range(2)]
        deg = [sb(f"deg{i}", [P, 2 * T]) for i in range(2)]
        xT = [sb(f"xT{i}", [128, B]) for i in range(4)]
        h1 = [[sb(f"h1{i}{e}", [128, B]) for e in range(2)] for i in range(2)]
        h0 = sb("h0", [128, B])
        weight = sb("weight", [P, T])
        base, diff, both, sqdiff = (sb(n, [P, T, D]) for n in ("base", "diff", "both", "sqdiff"))
        ids_in = [sem(f"ids_in{i}") for i in range(2)]
        xs_in = [sem(f"xs_in{i}") for i in range(2)]
        ga_in = [pool_sem(f"ga_in{i}") for i in range(2)]
        h_stored = [sem(f"h_stored{i}") for i in range(2)]
        deg_stored = [sem(f"deg_stored{i}") for i in range(2)]
        cleared_next = sem("cleared_next")
        t_done, t_copied = sem("t_done"), sem("t_copied")
        mm_done, mm_read = sem("mm_done"), sem("mm_read")
        exp_done, ln_done, low_done = sem("exp_done"), sem("ln_done"), sem("low_done")
        deg_done, w_part, w_done = sem("deg_done"), sem("w_part"), sem("w_done")
        diff_done, sq_done, corr_mm, corr_read = sem("diff_done"), sem("sq_done"), sem("corr_mm"), sem("corr_read")
        sp_began, pool_began = sem("sp_began"), sem("pool_began")
        J, K = 4, 5
        banks = Banks(m, K, mm_read)
        src_v, dst_v = (a[k].rearrange("(g t p) -> g p t", t=T, p=P) for k in ("src", "dst"))
        zero_v = m.table[2][0:N, :].rearrange("(g p r) n -> g p (r n)", p=P, r=16)
        block = ctx.enter_context(nc.Block())

        @block.sync
        def _(sp):
            def until(signal, value):
                sp.wait_ge(signal, value)
                settled(sp, sp_began)

            def load(g, par):
                if not (isinstance(g, int) and g < 2):
                    until(ga_in[par], nth(128, g, par) - 128)
                    until(t_done, J * (g - 1))
                sp.dma_start(ids[par][:, 0:T], src_v[bass.ds(g, 1), :, :].rearrange("g p t -> (g p) t"),
                             allow_slow_non_contiguous=True).then_inc(ids_in[par], 16)
                sp.dma_start(ids[par][:, T:2 * T], dst_v[bass.ds(g, 1), :, :].rearrange("g p t -> (g p) t"),
                             allow_slow_non_contiguous=True).then_inc(ids_in[par], 16)
                sp.dma_start(xs[par][:, :, :].rearrange("p t n -> p (t n)"),
                             m.state[0][bass.ds(g, 1), :, :].rearrange("g p n -> (g p) n")).then_inc(xs_in[par], 16)

            def store(g, par):
                sp.dma_start(zero_v[bass.ds(g, 1), :, :].rearrange("g p n -> (g p) n"),
                             m.zero[0:P, :]).then_inc(cleared_next, 16)
                until(deg_done, g + 1)
                sp.dma_start(m.degree[bass.ds(g, 1), :, :].rearrange("g p n -> (g p) n"),
                             deg[par][:, :]).then_inc(deg_stored[par], 16)
                for e, k in ((0, 1), (1, 2)):
                    until(mm_read, K * g + k + 1)
                    sp.dma_start(m.slot_hidden[bass.ds(2 * g + e, 1), :, :].rearrange("g p n -> (g p) n"),
                                 h1[par][e][:, :]).then_inc(h_stored[par], 16)
            load(0, 0)
            load(1, 1)
            with sp.Fori(0, G - 3, 2) as g:
                store(g, 0)
                load(g + 2, 0)
                store(g + 1, 1)
                load(g + 3, 1)
            store(G - 3, 0)
            load(G - 1, 0)
            store(G - 2, 1)
            store(G - 1, 0)
            for par, n in ((0, (G + 1) // 2), (1, G // 2)):
                sp.wait_ge(h_stored[par], 32 * n)
                sp.wait_ge(deg_stored[par], 16 * n)
            sp.wait_ge(cleared_next, 16 * G)

        @block.gpsimd
        def _(pool):
            clear_spent(pool, m)

            def step(g, par):
                pool.wait_ge(ids_in[par], nth(32, g, par))
                if not (isinstance(g, int) and g < 2):
                    pool.wait_ge(t_done, J * (g - 1))
                    pool.wait_ge(deg_done, g - 1)
                settled(pool, pool_began)
                for k in range(2 * T):
                    pool.indirect_dma_start(out=ga[par][:, k, :], out_offset=None, in_=m.table[0][:, :],
                                            in_offset=index(ids[par][:, k:k + 1].bitcast(U32))).then_inc(ga_in[par], 16)

            def squares(g):
                pool.wait_ge(mm_read, K * g + 5)
                pool.wait_ge(corr_mm, 2 * g)
                nc.gpsimd.tensor_tensor(sqdiff[:, :, :], diff[:, :, :], both[:, :, :], ALU.mult).then_inc(sq_done, 1)
            step(0, 0)
            step(1, 1)
            squares(0)
            with pool.Fori(2, G - 1, 2) as g:
                step(g, 0)
                squares(g - 1)
                step(g + 1, 1)
                squares(g)
            step(G - 1, 0)
            squares(G - 2)
            squares(G - 1)

        @block.tensor
        def _(pe):
            def turn(g, k, tiles):
                pe.wait_ge(t_copied, J * g + k + 1)
                for j in range(T):
                    last = nc.tensor.transpose(m.pt[k % 2][:, j * P:(j + 1) * P], tiles(j), m.ident[0:P, 0:P])
                last.then_inc(t_done, 1)

            def hidden(g, k, x, sums=None):
                banks.free(pe, g, k)
                last = nc.tensor.matmul(banks.bank(k)[:, 0:B], m.u1[:, 0, :], xT[x][:, :], start=True, stop=sums is None)
                if sums is not None:
                    last = nc.tensor.matmul(banks.bank(k)[:, 0:B], m.u1[:, 1, :], xT[sums][:, :], start=False, stop=True)
                last.then_inc(mm_done, 1)

            def output(g, k, hid):
                pe.wait_ge(mm_read, K * g + k - 3 + 1)
                banks.free(pe, g, k)
                for j in range(T):
                    last = nc.tensor.matmul(banks.bank(k)[0:P, j * D:(j + 1) * D], hid[:, j * P:(j + 1) * P], m.u2[:, :],
                                            start=True, stop=True)
                last.then_inc(mm_done, 1)

            def correct(g):
                pe.wait_ge(w_done, g + 1)
                pe.wait_ge(sq_done, g + 1)
                pe.wait_ge(corr_read, g)
                for i, x in enumerate((diff, sqdiff)):
                    for j in range(T):
                        last = nc.tensor.matmul(m.pz[:, i:i + 1], x[:, j, :], weight[:, j:j + 1],
                                                start=(j == 0), stop=(j == T - 1))
                    last.then_inc(corr_mm, 1)

            def step(g, par):
                pe.wait_ge(xs_in[par], nth(16, g, par))
                turn(g, 0, lambda j: xs[par][:, j, :])
                pe.wait_ge(ga_in[par], nth(128, g, par))
                turn(g, 1, lambda j: ga[par][:, j, 0:D])
                pe.wait_ge(t_copied, J * g + 0 + 3)
                hidden(g, 0, 0)
                turn(g, 2, lambda j: xs[par][:, T + j, :])
                pe.wait_ge(t_copied, J * g + 1 + 3)
                hidden(g, 1, 0, 1)
                turn(g, 3, lambda j: ga[par][:, T + j, 0:D])
                pe.wait_ge(t_copied, J * g + 3 + 3)
                hidden(g, 2, 2, 3)
                if not (isinstance(g, int) and g == 0):
                    correct(g - 1)
                output(g, 3, h0)
                output(g, 4, h1[par][0])
            each_step(pe, step)
            correct(G - 1)

        @block.scalar
        def _(act):
            nc.scalar.preload_act_table_set(TABLES)
            act.sem_inc(t_copied, 2)

            def copy(g, k):
                act.wait_ge(t_done, J * g + k + 1)
                act.wait_ge(mm_done, K * g)
                nc.scalar.copy(xT[k][:, :], m.pt[k % 2][:, 0:B]).then_inc(t_copied, 1)

            def softplus(g, k, buf):
                act.wait_ge(mm_done, K * g + k + 1)
                act_softplus(nc, act, exp_done, 3 * g + k + 1, banks.bank(k)[:, 0:B], buf, m.b_ub1).then_inc(ln_done, 1)

            def step(g, par):
                copy(g, 0)
                copy(g, 1)
                softplus(g, 0, h0[:, :])
                act.wait_ge(h_stored[par], nth(32, g, par) - 32)
                copy(g, 2)
                softplus(g, 1, h1[par][0][:, :])
                copy(g, 3)
                softplus(g, 2, h1[par][1][:, :])
            each_step(act, step)

        @block.vector
        def _(dve):
            def finish(g, k, buf):
                dve.wait_ge(ln_done, 3 * g + k + 1)
                dve_softplus(nc, dve, low_done, 3 * g + k + 1, banks.bank(k)[:, 0:B], buf, m.b_ub1).then_inc(mm_read, 1)

            def correct(g):
                dve.wait_ge(corr_mm, 2 * (g + 1))
                nc.vector.tensor_tensor(m.corr[:, :], m.corr[:, :], m.pz[:, 0:2], ALU.add).then_inc(corr_read, 1)
                dve.wait_ge(corr_read, g + 1)

            def step(g, par):
                dve.wait_ge(ga_in[par], nth(128, g, par))
                dve.wait_ge(deg_stored[par], nth(16, g, par) - 16)
                nc.vector.tensor_copy(deg[par][:, :], ga[par][:, :, D]).then_inc(deg_done, 1)
                finish(g, 0, h0[:, :])
                finish(g, 1, h1[par][0][:, :])
                if not (isinstance(g, int) and g == 0):
                    correct(g - 1)
                nc.vector.tensor_scalar(weight[:, :], deg[par][:, 0:T], 1.0, None, ALU.max).then_inc(w_part, 1)
                dve.wait_ge(w_part, g + 1)
                nc.vector.reciprocal(weight[:, :], weight[:, :]).then_inc(w_done, 1)
                finish(g, 2, h1[par][1][:, :])
                u0, u1 = (banks.bank(k)[0:P, :].rearrange("p (t n) -> p t n", t=T) for k in (3, 4))
                dve.wait_ge(mm_done, K * g + 4)
                nc.vector.tensor_copy(base[:, :, :], u0).then_inc(mm_read, 1)
                dve.wait_ge(mm_done, K * g + 5)
                dve.wait_ge(mm_read, K * g + 4)
                nc.vector.tensor_tensor(diff[:, :, :], u1, base[:, :, :], ALU.subtract).then_inc(diff_done, 1)
                nc.vector.tensor_tensor(both[:, :, :], u1, base[:, :, :], ALU.add).then_inc(mm_read, 1)
            each_step(dve, step)
            correct(G - 1)


def batch_norm(nc, m):
    with ExitStack() as ctx:
        sb, sem, pool_sem = allocate(nc, m, ctx, "bn")
        v = sb("v", [128, 12])
        diag = sb("diag", [128, 2, D])
        row = sb("row", [128, D])
        tmp_b = sb("tmp_b", [128, 2 * D], BF16)
        tmp_f = sb("tmp_f", [128, 2 * D])
        chain, var_done, log_done, std_done = sem("chain"), sem("var_done"), sem("log_done"), sem("std_done")
        diag_done, spread = sem("diag_done"), sem("spread")
        block = ctx.enter_context(nc.Block())
        c = {name: v[:, i:i + 1] for i, name in enumerate(
            ("mean", "var", "c1", "c2", "sq", "log", "rstd", "scale", "bias", "mu"))}

        @block.vector
        def _(dve):
            n = 0

            def link(ins):
                nonlocal n
                n += 1
                ins.then_inc(chain, 1)
                dve.wait_ge(chain, n)

            def tt(o, x, y, op):
                link(nc.vector.tensor_tensor(c[o], c[x], c[y], op))
            link(nc.vector.bn_aggr(v[:, 0:2], m.stats[:, :, :].rearrange("p a b -> p (a b)")))
            link(nc.vector.tensor_scalar(v[:, 2:4], m.corr[:, :], 1.0 / N, None, ALU.mult))
            tt("sq", "mean", "mean", ALU.mult)
            tt("var", "var", "sq", ALU.add)
            tt("var", "var", "c2", ALU.add)
            tt("mean", "mean", "c1", ALU.add)
            tt("sq", "mean", "mean", ALU.mult)
            link(nc.vector.tensor_tensor(c["var"], c["var"], c["sq"], ALU.subtract))
            link(nc.vector.tensor_scalar(c["var"], c["var"], 0.0, None, ALU.max))
            dve.sem_inc(var_done, 1)
            dve.wait_ge(std_done, 1)
            tt("scale", "rstd", "rstd", ALU.max)
            link(nc.vector.tensor_tensor(c["scale"], c["rstd"], m.gamma, ALU.mult))
            link(nc.vector.tensor_tensor(c["mu"], c["mean"], m.ub2, ALU.add))
            link(nc.vector.tensor_tensor(c["bias"], m.ub2, c["mu"], ALU.subtract))
            tt("bias", "bias", "scale", ALU.mult)
            link(nc.vector.tensor_tensor(c["bias"], c["bias"], m.beta, ALU.add))
            link(nc.vector.tensor_scalar(diag[:, 0, :], m.ident[:, :], c["scale"], None, ALU.mult))
            nc.vector.tensor_scalar(diag[:, 1, :], m.ident[:, :], c["bias"], None, ALU.mult).then_inc(diag_done, 1)
            dve.wait_ge(spread, 1)
            link(nc.vector.tensor_tensor(m.u2s[:, :], m.u2[:, :], m.pm[0][:, 0:D], ALU.mult))
            link(nc.vector.tensor_copy(row[:, :], m.pm[0][:, D:2 * D]))
            split_row(nc, dve, link, m, row[:, :], m.l0row, tmp_b, tmp_f)

        @block.scalar
        def _(act):
            nc.scalar.preload_act_table_set(TABLES)
            act.wait_ge(var_done, 1)
            nc.scalar.activation(c["log"], c["var"], ACT.Ln, bias=m.eps[:, :]).then_inc(log_done, 1)
            act.wait_ge(log_done, 1)
            nc.scalar.activation(c["rstd"], c["log"], ACT.Exp, scale=-0.5).then_inc(std_done, 1)

        @block.tensor
        def _(pe):
            pe.wait_ge(diag_done, 1)
            nc.tensor.matmul(m.pm[0][:, 0:2 * D], m.ones[:, :], diag[:, :, :].rearrange("p a b -> p (a b)"),
                             start=True, stop=True).then_inc(spread, 1)


def dense_plan(phase):
    return {1: [(0, 0, False), (1, 1, False)], 2: [(2, 0, True)], 3: [(3, 1, True)], 4: []}[phase]


def layers(nc, m, a, phase, out):
    plan = dense_plan(phase)
    S = len(plan)
    with ExitStack() as ctx:
        sb, sem, pool_sem = allocate(nc, m, ctx, f"l{phase}")
        ends = [("end", e) for e in range(2)]
        nodes = [("node", s, l) for s in range(S) for l in (3, 2, 1, 0)]
        if S == 2:
            units = [ends[0]] + nodes[0:4] + [ends[1]] + nodes[4:8]
        elif S == 1:
            units = ends + nodes
        else:
            units = ends
        U = len(units)

        def turns_of(u):
            if u[0] == "node":
                return [("x", u)] if u[2] else []
            return {1: [], 2: [("x", u), ("sum", u)], 3: [("x", u)], 4: [("emb", u)]}[phase]
        order = []
        summing = 1 if S == 2 else 2
        rels = [("rel", j, h) for j in range(T) for h in range(2)]
        after = {
            1: {},
            2: {1: [("turn", ("msg", 0))], 2: rels[0:2], 3: rels[2:4], 4: rels[4:6], 5: rels[6:8]},
            3: {2: [("turn", ("msg", 0)), ("turn", ("msg", 1))], 3: [("z",)], 4: [("logit",)], 5: [("weigh",)]},
            4: {}}[phase]
        if not S:
            order += [("turn", t) for t in turns_of(units[0])]
        for n, u in enumerate(units):
            if n + 1 < U:
                order += [("turn", t) for t in turns_of(units[n + 1])]
            elif S:
                order += [("ahead",)]
            if n == 0 and S:
                order += [("last",)]
            order += [("y", u)]
            if n:
                order += [("norm", units[n - 1])]
            order += [("stat", u)]
            if phase < 4:
                pieces = (({1: 5, 2: 1, 3: 2}[phase], ("same",)), (summing, ("sum",)), (3, ("count",)), (4, ("lead",)))
                order += [piece for at, piece in pieces if at == n]
            if phase > 1 and u == ends[1]:
                order += [("prepare",)]
            order += after.get(n, [])
        order += [("bias",)] if S else [("norm", units[-1])]
        early = turns_of(units[0]) if S else []
        jobs = early + [p[1] for p in order if p[0] == "turn"]
        prods = [p[1] if p[0] == "y" else p for p in order if p[0] in ("y", "rel", "z")]
        J, K = max(len(jobs), 1), len(prods)
        normed = units

        ids = [sb(f"ids{i}", [P, 2 * T], I32) for i in range(2)]
        xs = [sb(f"xs{i}", [P, 2 * T, D]) for i in range(2)]
        xo = [sb(f"xo{i}", [P, 2 * T, D]) for i in range(2)]
        if phase > 1:
            ga = [sb(f"ga{i}", [P, 2 * T, AW]) for i in range(2)]
            factor = sb("factor", [P, 2, 2 * T])
        if phase in (2, 4):
            deg = [sb(f"deg{i}", [P, 2 * T]) for i in range(2)]
        if phase == 1:
            hs = [[sb(f"hs{i}{e}", [128, B]) for e in range(2)] for i in range(2)]
        if phase == 2:
            kinds = [sb(f"kinds{i}", [P, T], I32) for i in range(2)]
            kindf, kmask = sb("kindf", [P, T]), sb("kmask", [P, T, R])
            prod = [sb(f"prod{i}", [P, R, D]) for i in range(2)]
        if phase == 3:
            hid = sb("hid", [128, B])
            gate = sb("gate", [P, T])
        if phase == 4:
            emb = sb("emb", [P, 2 * T, D])
        xT = {t: sb(f"xT{i}", [128, B]) for i, t in enumerate(jobs)}
        if phase < 4:
            if phase > 1:
                msg = sb("msg", [P, T, AW])
            sums = [sb(f"sums{i}", [P, T, AW]) for i in range(2)]
        rows = [sb(f"rows{i}", [P, 2 * T], I32) for i in range(2)]
        st, mv = sb("st", [P, U, T, 6]), sb("mv", [P, U, T, 2])
        logv, rstd, bias = (sb(x, [P, U, T]) for x in ("logv", "rstd", "bias"))
        width = D if phase == 1 else AW

        ids_in = [sem(f"ids_in{i}") for i in range(2)]
        rows_in = [sem(f"rows_in{i}") for i in range(2)]
        xs_in = [sem(f"xs_in{i}") for i in range(2)]
        ga_in = [pool_sem(f"ga_in{i}") for i in range(2)] if phase > 1 else None
        x_stored = [sem(f"x_stored{i}") for i in range(2)]
        nx_in = [sem(f"nx_in{i}") for i in range(2)] if S else None
        n_stored = [sem(f"n_stored{i}") for i in range(2)] if S else None
        lead_stored = [sem(f"lead_stored{i}") for i in range(2)] if phase == 2 else None
        cleared_next = sem("cleared_next") if phase == 1 else None
        summed = pool_sem("summed")
        t_done, t_copied = sem("t_done"), sem("t_copied")
        mm_done, mm_read = sem("mm_done"), sem("mm_read")
        st_done, mv_done, log_done, rstd_done, x_done = (sem(x) for x in ("st_done", "mv_done", "log_done",
                                                                          "rstd_done", "x_done"))
        pre_part, pre_done, y_part = (sem(x) for x in ("pre_part", "pre_done", "y_part"))
        msg_done, msg_part = sem("msg_done"), sem("msg_part")
        logit_mm, gate_arg, gate_exp = sem("logit_mm"), sem("gate_arg"), sem("gate_exp")
        sp_began, pool_began, dve_began = sem("sp_began"), sem("pool_began"), sem("dve_began")
        bias_done = sem("bias_done")
        dd = Dedupe(nc, m, sb, sem, lead=(phase == 2), width=width) if phase < 4 else None
        banks = Banks(m, K, mm_read)

        src_v, dst_v, kind_v = (a[k].rearrange("(g t p) -> g p t", t=T, p=P) for k in ("src", "dst", "edge_type_8"))
        xq = a["x"].rearrange("(g p q r) n -> q g p (r n)", p=P, q=Q, r=T)
        oq = out.rearrange("(g p q r) n -> q g p (r n)", p=P, q=Q, r=T)
        zero_v = m.table[3][0:N, :].rearrange("(g p r) n -> g p (r n)", p=P, r=16)
        IDS = {1: 48, 2: 64, 3: 48, 4: 32}[phase]
        ROWS = 32 if phase == 4 else 16
        XS = {1: 48, 2: 32, 3: 16, 4: 32}[phase]

        def slot_par(s, par):
            _, first, flips = plan[s]
            return (first + par) % 2 if flips else first

        def x_of(u, par):
            if u[0] == "end":
                e = slice(T * u[1], T * (u[1] + 1))
                return xs[par][:, e, :], xo[par][:, e, :]
            p = slot_par(u[1], par)
            return m.xb[u[2]][p][:, :, :], m.xb[u[2] + 1][1 - p][:, :, :]

        def layer_of(u):
            return phase - 1 if u[0] == "end" else u[2]

        def message(par):
            return xo[par][:, T:2 * T, :] if phase == 1 else msg[:, :, :]

        def count(seq, item, g):
            return len(seq) * g + seq.index(item) + 1

        def read(item, g):
            return K * g + prods.index(item) + 1 if item in prods else J * g + jobs.index(item) + 3

        def bank_of(item):
            return banks.bank(prods.index(item))

        def nodes_wait(eng, g, par, u):
            p = slot_par(u[1], par)
            if S == 2:
                eng.wait_ge(nx_in[p], 32 * (g + 1))
            else:
                eng.wait_ge(nx_in[p], nth(32, g, par))

        block = ctx.enter_context(nc.Block())

        @block.sync
        def _(sp):
            def until(signal, value):
                sp.wait_ge(signal, value)
                settled(sp, sp_began)

            def whole(t, g):
                return t[bass.ds(g, 1), :, :].rearrange("g p n -> (g p) n")

            def flat(t):
                return t.rearrange("p t n -> p (t n)")

            def load(g, par):
                if not (isinstance(g, int) and g < 2):
                    until(mm_read, read(("end", 1), g - 2))
                    if phase < 4:
                        until(dd.same_done, g - 1)
                sp.dma_start(ids[par][:, 0:T], src_v[bass.ds(g, 1), :, :].rearrange("g p t -> (g p) t"),
                             allow_slow_non_contiguous=True).then_inc(ids_in[par], 16)
                sp.dma_start(ids[par][:, T:2 * T], dst_v[bass.ds(g, 1), :, :].rearrange("g p t -> (g p) t"),
                             allow_slow_non_contiguous=True).then_inc(ids_in[par], 16)
                if phase < 4:
                    keys = a["dst" if phase == 2 else "src"]
                    sp.dma_start(dd.krow[par][:, :], keys[bass.ds(B * g, B)].partition_broadcast(P)
                                 ).then_inc(ids_in[par], 16)
                if phase == 2:
                    sp.dma_start(kinds[par][:, :], kind_v[bass.ds(g, 1), :, :].rearrange("g p t -> (g p) t"),
                             allow_slow_non_contiguous=True).then_inc(ids_in[par], 16)
                sp.dma_start(flat(xs[par][:, :, :]), whole(m.state[phase - 1], g)).then_inc(xs_in[par], 16)
                if phase in (2, 4):
                    sp.dma_start(deg[par][:, :], whole(m.degree, g)).then_inc(xs_in[par], 16)
                if phase == 1:
                    for e in range(2):
                        sp.dma_start(hs[par][e][:, :], whole(m.slot_hidden, 2 * g + e)).then_inc(xs_in[par], 16)

            def load_rows(g, par):
                if phase == 2:
                    return
                if not (isinstance(g, int) and g < 2):
                    until(summed, (128 if phase == 4 else 64) * (g - 1))
                for e in range(2 if phase == 4 else 1):
                    sp.dma_start(rows[par][:, T * e:T * (e + 1)], whole(m.lead[e], g)).then_inc(rows_in[par], 16)

            def load_nodes(g, s, par):
                q, p = plan[s][0], slot_par(s, par)
                sp.dma_start(flat(m.xb[0][p][:, :, :]), whole(xq[q], g)).then_inc(nx_in[p], 16)
                sp.dma_start(m.hb[p][:, :], whole(m.hidden, Q * g + q)).then_inc(nx_in[p], 16)

            def store_nodes(g, s, par):
                if phase == 1:
                    at = (g - 2, 1) if s == 0 else (g - 1, 0)
                elif isinstance(g, int) and g < 3:
                    at = {2: ((G - 2, 1), (G - 1, 0), (G - 1, 1)), 3: tuple((G - 3 + i, 2) for i in range(3))}[phase][g]
                else:
                    at = (g - 3, phase)
                until(x_done, count(normed, ("node", s, 3), g))
                if phase > 1 or not (isinstance(g, int) and (g < 1 or (g < 2 and s == 0))):
                    p = slot_par(s, par)
                    sp.dma_start(whole(oq[at[1]], at[0]), flat(m.xb[4][1 - p][:, :, :])).then_inc(n_stored[p], 16)
                else:
                    sp.sem_inc(n_stored[slot_par(s, par)], 16)

            def step(g, par, nodes_next, load_next):
                def next_nodes(s):
                    if nodes_next is not None:
                        until(mm_read, read(("node", s, 0), g))
                        load_nodes(g + nodes_next, s, par if nodes_next == 2 else 1 - par)
                if phase == 1:
                    sp.dma_start(whole(zero_v, g), m.zero[0:P, :]).then_inc(cleared_next, 16)
                if S == 2:
                    store_nodes(g, 0, par)
                    next_nodes(0)
                if load_next:
                    load(g + 2, par)
                until(x_done, count(normed, ("end", 1), g))
                if phase < 4:
                    sp.dma_start(whole(m.state[phase], g), flat(xo[par][:, :, :])).then_inc(x_stored[par], 16)
                if S:
                    store_nodes(g, S - 1, par)
                    next_nodes(S - 1)
                if phase == 2:
                    until(dd.lidx_done, g + 1)
                    sp.dma_start(whole(m.lead[1], g), dd.lidx[par][:, :].bitcast(I32)).then_inc(lead_stored[par], 16)
                if not (isinstance(g, int) and (g == 0 or g == G - 1)):
                    load_rows(g + 1, 1 - par)
            ahead = 2 if S == 1 else 1
            load(0, 0)
            load(1, 1)
            load_rows(0, 0)
            load_rows(1, 1)
            for g in range(ahead if S else 0):
                for s in range(S):
                    load_nodes(g, s, g % 2)

            def one(g, par):
                nodes_next = ahead if S and g + ahead < G else None
                step(g, par, nodes_next, g + 2 < G)
            for g in range(4):
                one(g, g % 2)
            with sp.Fori(4, G - 3, 2) as g:
                step(g, 0, ahead if S else None, True)
                step(g + 1, 1, ahead if S else None, True)
            for g in range(G - 3, G):
                one(g, g % 2)
            for par, n in ((0, (G + 1) // 2), (1, G // 2)):
                if phase < 4:
                    sp.wait_ge(x_stored[par], 16 * n)
                if phase == 2:
                    sp.wait_ge(lead_stored[par], 16 * n)
            for p in range(2 if S else 0):
                sp.wait_ge(n_stored[p], 16 * sum(slot_par(s, g % 2) == p for g in range(G) for s in range(S)))
            if phase == 1:
                sp.wait_ge(cleared_next, 16 * G)

        @block.gpsimd
        def _(pool):
            clear_spent(pool, m)

            def gather(g, par, e):
                pool.wait_ge(ids_in[par], nth(IDS, g, par))
                if not (isinstance(g, int) and g < 2):
                    pool.wait_ge(mm_read, read(("end", 1), g - 2))
                settled(pool, pool_began)
                for k in range(T * e, T * e + T):
                    pool.indirect_dma_start(out=ga[par][:, k, :], out_offset=None, in_=m.table[phase - 1][:, :],
                                            in_offset=index(ids[par][:, k:k + 1].bitcast(U32))).then_inc(ga_in[par], 16)

            def scatter(g, par):
                pool.wait_ge(dd.sum_copied, 2 * (g + 1))
                if phase == 2:
                    pool.wait_ge(dd.lidx_done, g + 1)
                else:
                    pool.wait_ge(rows_in[par], nth(ROWS, g, par))
                pool.wait_ge(summed, 64 * g)
                settled(pool, pool_began)
                for j in range(T):
                    at = dd.lidx[par][:, j:j + 1] if phase == 2 else rows[par][:, j:j + 1].bitcast(U32)
                    pool.indirect_dma_start(out=m.table[phase][:, :], out_offset=index(at), in_=sums[par][:, j, :],
                                            in_offset=None, compute_op=ALU.add).then_inc(summed, 16)

            def finals(g, par, e):
                pool.wait_ge(x_done, count(normed, ("end", e), g))
                pool.wait_ge(rows_in[par], nth(ROWS, g, par))
                pool.wait_ge(summed, 128 * g + 64 * e)
                settled(pool, pool_began)
                for k in range(T * e, T * e + T):
                    pool.indirect_dma_start(out=out[:, :], out_offset=index(rows[par][:, k:k + 1].bitcast(U32)),
                                            in_=xo[par][:, k, :], in_offset=None, bounds_check=N - 1,
                                            oob_is_err=False).then_inc(summed, 16)

            def split(g, par):
                if phase == 1:
                    pool.wait_ge(x_done, count(normed, ("end", 1), g))
                    dd.pool_split(pool, g, xo[par][:, T:2 * T, :])
                else:
                    pool.wait_ge(msg_done, g + 1)
                    dd.pool_split(pool, g, msg[:, :, :])

            def turn(g, par, more=True):
                if phase == 4:
                    for e in range(2):
                        finals(g - 1, 1 - par, e)
                        if more:
                            gather(g + 2, par, e)
                    return
                split(g - 1, 1 - par)
                scatter(g - 1, 1 - par)
                if phase > 1 and more:
                    gather(g + 2, par, 0)
                    gather(g + 2, par, 1)
            if phase > 1:
                for g in range(3):
                    gather(g, g % 2, 0)
                    gather(g, g % 2, 1)
            turn(1, 1)
            turn(2, 0)
            with pool.Fori(3, G - 2, 2) as g:
                turn(g, 1)
                turn(g + 1, 0)
            turn(G - 2, 1, False)
            turn(G - 1, 0, False)
            if phase == 4:
                finals(G - 1, 0, 0)
                finals(G - 1, 0, 1)
                pool.wait_ge(summed, 128 * G)
            else:
                split(G - 1, 0)
                scatter(G - 1, 0)
                pool.wait_ge(summed, 64 * G)

        @block.tensor
        def _(pe):
            def turn(g, par, job):
                kind, u = job
                if kind == "msg":
                    pe.wait_ge(x_done, count(normed, ("end", u), g))
                    tiles = xo[par][:, T * u:T * (u + 1), :]
                elif kind == "sum":
                    pe.wait_ge(pre_done, g + 1)
                    tiles = ga[par][:, T * u[1]:T * (u[1] + 1), 0:D]
                elif kind == "emb":
                    pe.wait_ge(pre_done, g + 1)
                    tiles = emb[:, T * u[1]:T * (u[1] + 1), :]
                else:
                    if u[0] == "end":
                        pe.wait_ge(xs_in[par], nth(XS, g, par))
                    elif u[1] == 0:
                        if not (isinstance(g, int) and g == 0):
                            pe.wait_ge(x_done, count(normed, ("node", S - 1, u[2] - 1), g - 1))
                    else:
                        pe.wait_ge(x_done, count(normed, ("node", 0, u[2] - 1), g))
                    tiles = x_of(u, par)[0]
                pe.wait_ge(t_copied, J * g + jobs.index(job) + 1)
                bank = m.pt[(par * J + jobs.index(job)) % 2]
                for j in range(T):
                    last = nc.tensor.transpose(bank[:, j * P:(j + 1) * P], tiles[:, j, :], m.ident[0:P, 0:P])
                last.then_inc(t_done, 1)

            def product(g, item):
                banks.free(pe, g, prods.index(item))
                return bank_of(item)

            def y(g, par, u):
                l = layer_of(u)
                if l == 0:
                    if u[0] == "end":
                        pe.wait_ge(xs_in[par], nth(XS, g, par))
                        lhs = hs[par][u[1]]
                    else:
                        nodes_wait(pe, g, par, u)
                        lhs = m.hb[slot_par(u[1], par)]
                    pairs = [(lhs, m.u2s[:, :])]
                else:
                    w = {1: m.l1w[:, 0, :], 2: m.l2w[:, :], 3: m.wl[:, :]}[l]
                    pairs = [(xT[t], m.l1w[:, 1, :] if t[0] == "sum" else w) for t in turns_of(u)]
                    pe.wait_ge(t_copied, read(turns_of(u)[-1], g))
                bank = product(g, u)
                row = (m.l0row, m.l1row, m.l2row, m.l3row)[l]
                nc.tensor.matmul(bank[0:P, :], m.ones3[:, 0:P], row[:, :], start=True, stop=False)
                for i, (lhs, w) in enumerate(pairs):
                    for j in range(T):
                        last = nc.tensor.matmul(bank[0:P, j * D:(j + 1) * D], lhs[:, j * P:(j + 1) * P], w,
                                                start=False, stop=(i == len(pairs) - 1 and j == T - 1))
                last.then_inc(mm_done, 1)

            def step(g, par):
                for kind, *arg in order:
                    if kind == "turn":
                        turn(g, par, arg[0])
                    elif kind == "ahead" and not (isinstance(g, int) and g == G - 1):
                        for job in early:
                            turn(g + 1, 1 - par, job)
                    elif kind == "y":
                        y(g, par, arg[0])
                    elif kind == "count" and phase == 2:
                        dd.pe_count(pe, g, par)
                    elif kind == "sum" and not (isinstance(g, int) and g == 0):
                        dd.pe_sum(pe, g - 1, 1 - par, message(1 - par))
                    elif kind == "rel":
                        j, h = arg
                        pe.wait_ge(t_copied, read(("msg", 0), g))
                        bank = product(g, ("rel", j, h))
                        nc.tensor.matmul(bank[0:P, :], xT[("msg", 0)][:, j * P:(j + 1) * P],
                                         m.wrel[:, 4 * h:4 * h + 4, :].rearrange("p r n -> p (r n)"),
                                         start=True, stop=True).then_inc(mm_done, 1)
                    elif kind == "z":
                        pe.wait_ge(t_copied, read(("msg", 1), g))
                        bank = product(g, ("z",))
                        for e in range(2):
                            last = nc.tensor.matmul(bank[:, 0:B], m.v1[:, e, :], xT[("msg", e)][:, :], start=(e == 0),
                                                    stop=(e == 1))
                        last.then_inc(mm_done, 1)
                    elif kind == "logit":
                        pe.wait_ge(mm_read, read(("z",), g))
                        pe.wait_ge(gate_arg, g)
                        for j in range(T):
                            last = nc.tensor.matmul(m.pz[0:P, j:j + 1], hid[:, j * P:(j + 1) * P], m.v2[:, :],
                                                    start=True, stop=True)
                        last.then_inc(logit_mm, 1)
            for job in early:
                turn(0, 0, job)
            each_step(pe, step)
            if phase < 4:
                dd.pe_sum(pe, G - 1, 0, message(0))

        @block.scalar
        def _(act):
            nc.scalar.preload_act_table_set(TABLES)
            act.sem_inc(t_copied, 2)

            def copy(g, par, job):
                k = jobs.index(job)
                act.wait_ge(t_done, J * g + k + 1)
                if not (isinstance(g, int) and g == 0):
                    user = job[1] if job[0] != "msg" else ("z",) if phase == 3 else prods[-1]
                    act.wait_ge(mm_done, count(prods, user, g - 1))
                nc.scalar.copy(xT[job][:, :], m.pt[(par * J + k) % 2][:, 0:B]).then_inc(t_copied, 1)

            def norm(g, par, u):
                n = units.index(u)
                o = x_of(u, par)[1]
                act.wait_ge(bias_done, U * g + n + 1)
                for j in range(T):
                    last = nc.scalar.activation(o[:, j, :], o[:, j, :], ACT.Identity, bias=bias[:, n, j:j + 1],
                                                scale=rstd[:, n, j:j + 1])
                last.then_inc(x_done, 1)

            def step(g, par):
                for kind, *arg in order:
                    if kind == "turn":
                        copy(g, par, arg[0])
                    elif kind == "ahead" and not (isinstance(g, int) and g == G - 1):
                        for job in early:
                            copy(g + 1, 1 - par, job)
                    elif kind == "stat":
                        n = units.index(arg[0])
                        act.wait_ge(mv_done, U * g + n + 1)
                        nc.scalar.activation(logv[:, n, :], mv[:, n, :, 1], ACT.Ln, bias=m.eps[0:P, :]).then_inc(log_done, 1)
                        act.wait_ge(log_done, U * g + n + 1)
                        nc.scalar.activation(rstd[:, n, :], logv[:, n, :], ACT.Exp, scale=-0.5).then_inc(rstd_done, 1)
                    elif kind == "norm":
                        norm(g, par, arg[0])
                    elif kind == "last" and not (isinstance(g, int) and g == 0):
                        norm(g - 1, 1 - par, units[-1])
                    elif kind == "logit":
                        act.wait_ge(gate_arg, g + 1)
                        nc.scalar.activation(gate[:, :], gate[:, :], ACT.Exp, scale=-1.0).then_inc(gate_exp, 1)
                    elif kind == "sum" and not (isinstance(g, int) and g == 0):
                        copy_sums(g - 1, 1 - par)

            def copy_sums(g, par):
                if not (isinstance(g, int) and g < 2):
                    act.wait_ge(summed, 64 * (g - 1))
                dd.act_sum(act, g, sums[par])
            if phase == 1:
                for i in range(2):
                    nc.scalar.copy(sums[i][:, :, D:AW], m.zero[0:P, 0:T * (AW - D)].rearrange("p (t n) -> p t n", t=T))
            for job in early:
                copy(0, 0, job)
            each_step(act, step)
            if S:
                norm(G - 1, 0, units[-1])
            if phase < 4:
                copy_sums(G - 1, 0)

        @block.vector
        def _(dve):
            if phase in (2, 3):
                nc.vector.memset(msg[:, :, D:AW], 0.0).then_inc(msg_part, 1)
                dve.wait_ge(msg_part, 1)
            if phase == 2:
                nc.vector.memset(msg[:, :, D:D + 1], 1.0).then_inc(msg_part, 1)
                dve.wait_ge(msg_part, 2)

            def tile(t, u, j):
                return t[:, T * u[1] + j, :]

            def prepare(g, par):
                if phase == 1:
                    return
                parts = {2: 2, 3: 1, 4: 4}[phase]
                n = parts * g

                def part(ins):
                    nonlocal n
                    n = n + 1
                    ins.then_inc(pre_part, 1)
                    dve.wait_ge(pre_part, n)
                dve.wait_ge(ga_in[par], nth(128, g, par))
                if phase in (2, 4):
                    dve.wait_ge(xs_in[par], nth(XS, g, par))
                f0, f1 = factor[:, 0, :], factor[:, 1, :]
                if phase == 2:
                    part(nc.vector.tensor_scalar(f0, deg[par][:, :], 1.0, None, ALU.max))
                    part(nc.vector.reciprocal(f0, f0))
                    for k in range(2 * T):
                        last = nc.vector.tensor_scalar(ga[par][:, k, 0:D], ga[par][:, k, 0:D], f0[:, k:k + 1], None,
                                                       ALU.mult)
                    last.then_inc(pre_done, 1)
                elif phase == 3:
                    part(nc.vector.tensor_scalar(f0, ga[par][:, :, D], 1.0, None, ALU.max))
                    nc.vector.reciprocal(f0, f0).then_inc(pre_done, 1)
                    dve.wait_ge(pre_done, g + 1)
                elif phase == 4:
                    part(nc.vector.tensor_scalar(f1, ga[par][:, :, D], 1e-9, None, ALU.add))
                    part(nc.vector.reciprocal(f1, f1))
                    part(nc.vector.tensor_scalar(f0, deg[par][:, :], 0.0, 0.5, ALU.is_gt, ALU.mult))
                    part(nc.vector.tensor_tensor(f1, f1, f0, ALU.mult))
                    nc.vector.tensor_scalar(f0, f0, -1.0, 1.0, ALU.mult, ALU.add).then_inc(y_part, 1)
                    dve.wait_ge(y_part, 2 * g + 1)
                    dve.wait_ge(t_done, J * g)
                    for k in range(2 * T):
                        last = nc.vector.tensor_scalar(emb[:, k, :], xs[par][:, k, :], f0[:, k:k + 1], None, ALU.mult)
                    last.then_inc(y_part, 1)
                    dve.wait_ge(y_part, 2 * g + 2)
                    for k in range(2 * T):
                        last = nc.vector.scalar_tensor_tensor(emb[:, k, :], ga[par][:, k, 0:D], f1[:, k:k + 1],
                                                              emb[:, k, :], ALU.mult, ALU.add)
                    last.then_inc(pre_done, 1)

            def y(g, par, u):
                l = layer_of(u)
                x, o = x_of(u, par)
                bank = bank_of(u)[0:P, :].rearrange("p (t n) -> p t n", t=T)
                dve.wait_ge(mm_done, count(prods, u, g))
                if u[0] == "end":
                    dve.wait_ge(xs_in[par], nth(XS, g, par))
                    if phase < 4:
                        dve.wait_ge(x_stored[par], nth(16, g, par) - 16)
                    if phase == 4 and not (isinstance(g, int) and g < 2):
                        dve.wait_ge(summed, 128 * (g - 1))
                    if phase == 1 and not (isinstance(g, int) and g < 2):
                        dve.wait_ge(dd.sum_mm, g - 1)
                else:
                    if u[2] == 0:
                        nodes_wait(dve, g, par, u)
                    if u[2] == 3:
                        if S == 2:
                            dve.wait_ge(n_stored[slot_par(u[1], par)], 16 * g)
                        else:
                            dve.wait_ge(n_stored[slot_par(u[1], par)], nth(16, g, par) - 16)
                    else:
                        if u[1] == 0:
                            dve.wait_ge(t_done, J * g)
                        else:
                            dve.wait_ge(t_done, count(jobs, ("x", ("node", 0, u[2] + 1)), g))
                if l < 2:
                    nc.vector.tensor_tensor(o, bank, x, ALU.add).then_inc(mm_read, 1)
                else:
                    if l == 2 and u[0] == "end":
                        for j in range(T):
                            last = nc.vector.scalar_tensor_tensor(bank[:, j, :], tile(ga[par], u, j)[:, 0:D],
                                                                  factor[:, 0, T * u[1] + j:T * u[1] + j + 1],
                                                                  bank[:, j, :], ALU.mult, ALU.add)
                        last.then_inc(y_part, 1)
                        dve.wait_ge(y_part, 2 * g + u[1] + 1)
                    nc.vector.scalar_tensor_tensor(o, bank, 0.0, x, ALU.max, ALU.add).then_inc(mm_read, 1)

            def norm(g, u):
                n = units.index(u)
                dve.wait_ge(rstd_done, U * g + n + 1)
                nc.vector.scalar_tensor_tensor(bias[:, n, :], mv[:, n, :, 0], -1.0, rstd[:, n, :], ALU.mult,
                                               ALU.mult).then_inc(bias_done, 1)

            def step(g, par):
                for kind, *arg in order:
                    if kind == "same":
                        if phase == 2:
                            dve.wait_ge(ids_in[par], nth(IDS, g, par))
                            nc.vector.tensor_copy(kindf[:, :], kinds[par][:, :]).then_inc(msg_part, 1)
                            dve.wait_ge(msg_part, 5 * g + 3)
                            nc.vector.tensor_tensor(kmask[:, :, :], kindf[:, :].unsqueeze(2).to_broadcast([P, T, R]),
                                                    m.relation[:, :].unsqueeze(1).to_broadcast([P, T, R]),
                                                    ALU.is_equal).then_inc(msg_part, 1)
                            dve.wait_ge(msg_part, 5 * g + 4)
                        dve.wait_ge(ids_in[par], nth(IDS, g, par))
                        dd.dve_same(dve, g, par, ids[par][:, T:2 * T] if phase == 2 else ids[par][:, 0:T])
                    elif kind == "lead":
                        if phase == 2:
                            dd.dve_lead(dve, g, par, lead_stored[par], summed)
                    elif kind == "y":
                        y(g, par, arg[0])
                    elif kind == "stat":
                        u, n = arg[0], units.index(arg[0])
                        o = x_of(u, par)[1]
                        dve.wait_ge(mm_read, read(u, g))
                        for j in range(T):
                            last = nc.vector.bn_stats(st[:, n, j, :], o[:, j, :])
                        last.then_inc(st_done, 1)
                        dve.wait_ge(st_done, U * g + n + 1)
                        settled(dve, dve_began)
                        for j in range(T):
                            last = nc.vector.bn_aggr(mv[:, n, j, :], st[:, n, j, :])
                        last.then_inc(mv_done, 1)
                    elif kind == "norm":
                        norm(g, arg[0])
                    elif kind == "bias":
                        norm(g, units[-1])
                    elif kind == "prepare" and not (isinstance(g, int) and g == G - 1):
                        dve.wait_ge(mm_read, read(("end", 1), g))
                        prepare(g + 1, 1 - par)
                    elif kind == "rel":
                        j, h = arg
                        item = ("rel", j, h)
                        bank = bank_of(item)[0:P, :].rearrange("p (r n) -> p r n", r=4)
                        dve.wait_ge(mm_done, count(prods, item, g))
                        if h == 0:
                            if j == 1:
                                dve.wait_ge(msg_done, g)
                            else:
                                dve.wait_ge(msg_part, 5 * g + (5 if j == 2 else 6 if j == 3 else 4))
                        nc.vector.tensor_tensor(prod[j % 2][:, 4 * h:4 * h + 4, :], bank,
                                                kmask[:, j, 4 * h:4 * h + 4].unsqueeze(2).to_broadcast([P, 4, D]),
                                                ALU.mult).then_inc(mm_read, 1)
                        if h == 1:
                            dve.wait_ge(mm_read, read(item, g))
                            if j == 0:
                                dve.wait_ge(dd.sum_mm, g)
                            ins = nc.vector.tensor_reduce(msg[:, j, 0:D], prod[j % 2][:, :, :].rearrange("p r n -> p n r"),
                                                          mybir.AxisListType.X, ALU.add)
                            ins.then_inc(msg_done if j == T - 1 else msg_part, 1)
                    elif kind == "z":
                        bank = bank_of(("z",))[:, 0:B]
                        dve.wait_ge(mm_done, count(prods, ("z",), g))
                        dve.wait_ge(logit_mm, g)
                        nc.vector.tensor_scalar(hid[:, :], bank, m.b_v1, 0.0, ALU.add, ALU.max).then_inc(mm_read, 1)
                    elif kind == "logit":
                        dve.wait_ge(logit_mm, g + 1)
                        nc.vector.tensor_scalar(gate[:, :], m.pz[0:P, 0:T], m.nb2[0:P, :], -80.0, ALU.subtract,
                                                ALU.max).then_inc(gate_arg, 1)
                    elif kind == "weigh":
                        dve.wait_ge(gate_exp, g + 1)
                        dve.wait_ge(dd.sum_mm, g)
                        nc.vector.tensor_scalar(gate[:, :], gate[:, :], 1.0, None, ALU.add).then_inc(msg_part, 1)
                        dve.wait_ge(msg_part, 2 * g + 2)
                        nc.vector.reciprocal(gate[:, :], gate[:, :]).then_inc(msg_part, 1)
                        dve.wait_ge(msg_part, 2 * g + 3)
                        nc.vector.tensor_copy(msg[:, :, D], gate[:, :])
                        dve.wait_ge(x_done, count(normed, ("end", 1), g))
                        for j in range(T):
                            last = nc.vector.tensor_scalar(msg[:, j, 0:D], xo[par][:, T + j, :], gate[:, j:j + 1], None,
                                                           ALU.mult)
                        last.then_inc(msg_done, 1)
            prepare(0, 0)
            each_step(dve, step)


def drain(nc, m, out):
    with ExitStack() as ctx:
        sb, sem, pool_sem = allocate(nc, m, ctx, "dr")
        units = [(t, l) for t in range(3) for l in range(3, t, -1)]
        xT = [sb(f"xT{i}", [128, B]) for i in range(len(units))]
        st, mv = sb("st", [P, T, 6]), sb("mv", [P, T, 2])
        logv, rstd = sb("logv", [P, T]), sb("rstd", [P, T])
        t_done, t_copied, mm_done, y_done = sem("t_done"), sem("t_copied"), sem("mm_done"), sem("y_done")
        st_done, mv_done, log_done, rstd_done, x_done = (sem(x) for x in ("st_done", "mv_done", "log_done",
                                                                          "rstd_done", "x_done"))
        stored = sem("stored")
        oq = out.rearrange("(g p q r) n -> q g p (r n)", p=P, q=Q, r=T)
        block = ctx.enter_context(nc.Block())

        def x_of(t, l):
            return m.xb[l][t % 2], m.xb[l + 1][1 - t % 2]

        @block.sync
        def _(sp):
            for n, (t, l) in enumerate(units):
                if l == 3:
                    sp.wait_ge(x_done, n + 1)
                    sp.dma_start(oq[Q - 1, G - 3 + t], x_of(t, l)[1][:, :, :].rearrange("p t n -> p (t n)")
                                 ).then_inc(stored, 16)
            sp.wait_ge(stored, 48)

        @block.tensor
        def _(pe):
            for n, (t, l) in enumerate(units):
                bank = m.pt[n % 2]
                if n:
                    pe.wait_ge(x_done, n)
                for j in range(T):
                    last = nc.tensor.transpose(bank[:, j * P:(j + 1) * P], x_of(t, l)[0][:, j, :], m.ident[0:P, 0:P])
                last.then_inc(t_done, 1)
                pe.wait_ge(t_copied, n + 1)
                row, w = {1: (m.l1row, m.l1w[:, 0, :]), 2: (m.l2row, m.l2w[:, :]), 3: (m.l3row, m.wl[:, :])}[l]
                bank = m.pm[n % 2]
                nc.tensor.matmul(bank[0:P, :], m.ones3[:, 0:P], row[:, :], start=True, stop=False)
                for j in range(T):
                    last = nc.tensor.matmul(bank[0:P, j * D:(j + 1) * D], xT[n][:, j * P:(j + 1) * P], w, start=False,
                                            stop=(j == T - 1))
                last.then_inc(mm_done, 1)

        @block.scalar
        def _(act):
            nc.scalar.preload_act_table_set(TABLES)
            for n, (t, l) in enumerate(units):
                act.wait_ge(t_done, n + 1)
                nc.scalar.copy(xT[n][:, :], m.pt[n % 2][:, 0:B]).then_inc(t_copied, 1)
                act.wait_ge(mv_done, n + 1)
                nc.scalar.activation(logv[:, :], mv[:, :, 1], ACT.Ln, bias=m.eps[0:P, :]).then_inc(log_done, 1)
                act.wait_ge(log_done, n + 1)
                nc.scalar.activation(rstd[:, :], logv[:, :], ACT.Exp, scale=-0.5).then_inc(rstd_done, 1)

        @block.vector
        def _(dve):
            for n, (t, l) in enumerate(units):
                x, o = x_of(t, l)
                bank = m.pm[n % 2][0:P, :].rearrange("p (t n) -> p t n", t=T)
                dve.wait_ge(mm_done, n + 1)
                if l == 3 and t == 2:
                    dve.wait_ge(stored, 48 - 16)
                if l == 1:
                    nc.vector.tensor_tensor(o[:, :, :], bank, x[:, :, :], ALU.add).then_inc(y_done, 1)
                else:
                    nc.vector.scalar_tensor_tensor(o[:, :, :], bank, 0.0, x[:, :, :], ALU.max, ALU.add
                                                   ).then_inc(y_done, 1)
                dve.wait_ge(y_done, n + 1)
                for j in range(T):
                    last = nc.vector.bn_stats(st[:, j, :], o[:, j, :])
                last.then_inc(st_done, 1)
                dve.wait_ge(st_done, n + 1)
                for j in range(T):
                    last = nc.vector.bn_aggr(mv[:, j, :], st[:, j, :])
                last.then_inc(mv_done, 1)
                dve.wait_ge(rstd_done, n + 1)
                for j in range(T):
                    last = nc.vector.tensor_scalar(o[:, j, :], o[:, j, :], mv[:, j, 0:1], rstd[:, j:j + 1],
                                                   ALU.subtract, ALU.mult)
                last.then_inc(x_done, 1)
                dve.wait_ge(x_done, n + 1)


def program(nc, a, out):
    m = Store()
    m.spent, m.fresh = [], []
    m.columns = ("L0_gnn_b1", "L0_gnn_ub1", "L3_gnn_b1", "L0_gnn_gamma", "L0_gnn_beta", "L0_gnn_ub2")
    with ExitStack() as ctx:
        m.ctx = ctx
        sb, sem, pool_sem = allocate(nc, m, ctx, "all")
        m.ident, m.ones = sb("ident", [128, D]), sb("ones", [128, D])
        m.ones3 = sb("ones3", [128, D], BF16)
        m.onesb = sb("onesb", [P, 1], BF16)
        m.before = sb("before", [P, P], BF16)
        m.w1, m.w2 = sb("w1", [128, 3, D]), sb("w2", [128, D])
        m.u1, m.u2, m.u2s = sb("u1", [128, 2, D]), sb("u2", [128, D]), sb("u2s", [128, D])
        m.l1w, m.l2w = sb("l1w", [128, 2, D]), sb("l2w", [128, D])
        m.wrel, m.v1, m.v2, m.wl = sb("wrel", [128, R, D]), sb("v1", [128, 2, D]), sb("v2", [128, 1]), sb("wl", [128, D])
        m.col = sb("col", [128, len(m.columns)])
        m.b_b1, m.b_ub1, m.b_v1, m.gamma, m.beta, m.ub2 = (m.col[:, i:i + 1] for i in range(6))
        m.nb2, m.eps = sb("nb2", [128, 1]), sb("eps", [128, 1])
        m.b2row, m.l0row, m.l1row, m.l2row, m.l3row = (sb(f"row{i}", [128, T * D], BF16) for i in range(5))
        m.corr = sb("corr", [128, 2])
        m.relation = sb("relation", [P, R])
        m.hb = [sb(f"hb{i}", [128, B]) for i in range(2)]
        m.xb = [[sb(f"xb{l}{i}", [P, T, D]) for i in range(2)] for l in range(5)]
        m.sink = sb("sink", [P, T])
        m.zero = sb("zero", [128, 16 * AW])
        m.stats = sb("stats", [128, Q * G, 6])
        m.pt = [ctx.enter_context(nc.psum_tensor(f"pt{i}", [128, 512], F32)) for i in range(2)]
        m.pm = [ctx.enter_context(nc.psum_tensor(f"pm{i}", [128, 512], F32)) for i in range(3)]
        m.pa = [ctx.enter_context(nc.psum_tensor(f"pa{i}", [128, 512], F32)) for i in range(2)]
        m.pz = ctx.enter_context(nc.psum_tensor("pz", [128, 512], F32))

        def dram(name, shape, dt=F32):
            return nc.dram_tensor(name, shape, dt, kind="Internal").ap()
        m.table = [dram(f"table{i}", (N + SINK, AW)) for i in range(4)]
        m.state = [dram(f"state{i}", (G, P, 2 * T * D)) for i in range(4)]
        m.hidden = dram("hidden", (Q * G, 128, B))
        m.slot_hidden = dram("slot_hidden", (2 * G, 128, B))
        m.lead = [dram(f"lead{i}", (G, P, T), I32) for i in range(2)]
        m.degree = dram("degree", (G, P, 2 * T))
        setup(nc, m, a)
        edges_mlp(nc, m, a)
        nodes_mlp(nc, m, a)
        batch_norm(nc, m)
        for phase in (1, 2, 3):
            layers(nc, m, a, phase, out)
        drain(nc, m, out)
        layers(nc, m, a, 4, out)

_INS = ['x', 'src', 'dst', 'edge_attr_128', 'edge_type_8', 'L0_gnn_W1', 'L0_gnn_b1', 'L0_gnn_W2', 'L0_gnn_b2',
        'L0_gnn_U1', 'L0_gnn_ub1', 'L0_gnn_U2', 'L0_gnn_ub2', 'L0_gnn_gamma', 'L0_gnn_beta', 'L1_gnn_W', 'L1_gnn_b',
        'L2_gnn_W_rel', 'L2_gnn_W_self_w', 'L2_gnn_W_self_b', 'L3_gnn_W1', 'L3_gnn_b1', 'L3_gnn_W2', 'L3_gnn_b2',
        'L3_gnn_Wl', 'L3_gnn_bl']


def kernel(**inputs):
    import numpy as _np
    import concourse.bacc as _bacc
    from concourse import mybir as _mybir
    from concourse.bass_utils import run_bass_kernel_spmd as _run

    nc = _bacc.Bacc("TRN2", target_bir_lowering=False, num_devices=1)
    arrays, args = {}, {}
    for name in _INS:
        arr = _np.ascontiguousarray(inputs[name])
        arrays[f"in_{name}"] = arr
        args[name] = nc.dram_tensor(f"in_{name}", arr.shape, _mybir.dt.from_np(arr.dtype), kind="ExternalInput").ap()
    out = nc.dram_tensor("out_0", (N, D), _mybir.dt.float32, kind="ExternalOutput").ap()
    program(nc, args, out)
    r = _run(nc, [arrays], core_ids=[0])
    return r.results[0]["out_0"]
```
